# Optimizing a Trainium2 kernel written in Bass

```python
import numpy as np
import jax
import jax.numpy as jnp

def _softmax(x, axis=-1):
    return jax.nn.softmax(x, axis=axis)

def _gelu(x):
    return jax.nn.gelu(x, approximate=True)

def _silu(x):
    return jax.nn.silu(x)

def _sigmoid(x):
    return jax.nn.sigmoid(x)

def _layernorm(x, axis=-1, eps=1e-05):
    m = jnp.mean(x, axis=axis, keepdims=True)
    v = jnp.var(x, axis=axis, keepdims=True)
    return (x - m) / jnp.sqrt(v + eps)

def _scatter_add(tgt, idx, src, axis=0):
    return tgt.at[idx].add(src)

def _segment_sum(src, seg, n):
    return jax.ops.segment_sum(src, seg, n)
kernel_name = 'mk_gnn_preln_d4_gnn_r32_2ae8ce'

def setup_inputs(seed: int=0):
    np.random.seed(seed)
    _w = jnp.asarray

    def _rec_inputs():
        import jax
        import jax.numpy as jnp
        _gk = jax.random.key(seed)
        x = -0.0003713 + 1 * jax.random.normal(jax.random.fold_in(_gk, 1), (3125, 128), jnp.float32)
        _s = jax.random.randint(jax.random.fold_in(_gk, 2), (25000,), 0, 3125, jnp.int32)
        _d = jax.random.randint(jax.random.fold_in(_gk, 3), (25000,), 0, 3125, jnp.int32)
        _loop = jnp.arange(3125, dtype=jnp.int32)
        src = jnp.concatenate([_s, _d, _loop])
        dst = jnp.concatenate([_d, _s, _loop])
        _o = jnp.argsort(dst, stable=True)
        src = src[_o]
        dst = dst[_o]
        edge_weight = jax.random.uniform(jax.random.fold_in(_gk, 15), (53125,), jnp.float32, 0.0, 1)
        return (x, src, dst, edge_weight)
    x, src, dst, edge_weight = _rec_inputs()

    def _L0_gnn_setup():
        import jax, jax.numpy as jnp
        import numpy as np
        N_NODES = 3125
        N_EDGES = 50000
        D_IN = 128
        D_OUT = 128
        key = jax.random.key(seed)
        k1, k2, k3, k4, k5, k6 = jax.random.split(key, 6)
        x = jax.random.normal(k1, (N_NODES, D_IN), dtype=jnp.float32)
        edge_src = jax.random.randint(k2, (N_EDGES,), 0, N_NODES, dtype=jnp.int64)
        edge_dst = jax.random.randint(k3, (N_EDGES,), 0, N_NODES, dtype=jnp.int64)
        edge_vals = jax.random.uniform(k4, (N_EDGES,), dtype=jnp.float32)
        W = jax.random.normal(k5, (D_OUT, D_IN), dtype=jnp.float32) / np.sqrt(D_IN)
        b = jax.random.normal(k6, (D_OUT,), dtype=jnp.float32) * 0.01
        return {'x': x, 'edge_src': edge_src, 'edge_dst': edge_dst, 'edge_vals': edge_vals, 'W': W, 'b': b}
    _L0_gnn_all = _L0_gnn_setup()
    _L0_gnn_in = {k: v for k, v in _L0_gnn_all.items() if k in ('W', 'b')}
    del _L0_gnn_all

    def _L1_gnn_setup():
        import jax, jax.numpy as jnp
        import numpy as np
        SDIM = 128
        DEPTH = 5
        CUTOFF = 5.0
        NUM_RADIAL = 32
        N_NODES = 50000
        N_EDGES = 12500

        def ssp(v):
            return jax.nn.softplus(v) - jnp.log(2.0).astype(v.dtype)
        key = jax.random.key(seed)
        ks = jax.random.split(key, 16)
        x = jax.random.normal(ks[0], (N_NODES, SDIM), dtype=jnp.float32)
        edge_index = jax.random.randint(ks[1], (2, N_EDGES), 0, N_NODES, dtype=jnp.int64)
        edge_attr = jax.random.uniform(ks[2], (N_EDGES,), dtype=jnp.float32)
        batch = jnp.sort(jax.random.randint(ks[3], (N_NODES,), 0, 64, dtype=jnp.int64))
        s = 1.0 / np.sqrt(SDIM)
        sr = 1.0 / np.sqrt(NUM_RADIAL)
        return {'x': x, 'edge_attr': edge_attr, 'fw1': jax.random.normal(ks[4], (DEPTH, NUM_RADIAL, SDIM), dtype=jnp.float32) * sr, 'fb1': jnp.zeros((DEPTH, SDIM), dtype=jnp.float32), 'fw2': jax.random.normal(ks[5], (DEPTH, SDIM, SDIM), dtype=jnp.float32) * s, 'fb2': jnp.zeros((DEPTH, SDIM), dtype=jnp.float32), 'lin1_w': jax.random.normal(ks[6], (DEPTH, SDIM, SDIM), dtype=jnp.float32) * s, 'lin2_w': jax.random.normal(ks[7], (DEPTH, SDIM, SDIM), dtype=jnp.float32) * s, 'lin2_b': jnp.zeros((DEPTH, SDIM), dtype=jnp.float32), 'ln_g': jnp.ones((DEPTH, SDIM), dtype=jnp.float32), 'ln_b': jnp.zeros((DEPTH, SDIM), dtype=jnp.float32), 'edge_index': edge_index, 'batch': batch}
    _L1_gnn_all = _L1_gnn_setup()
    _L1_gnn_in = {k: v for k, v in _L1_gnn_all.items() if k in ('fw1', 'fb1', 'fw2', 'fb2', 'lin1_w', 'lin2_w', 'lin2_b', 'ln_g', 'ln_b')}
    del _L1_gnn_all

    def _L2_gnn_setup():
        import jax, jax.numpy as jnp
        import numpy as np
        N, D, E = (3125, 128, 50000)
        key = jax.random.key(seed)
        k1, k2, k3, k4, k5, k6 = jax.random.split(key, 6)
        h = jax.random.normal(k1, (N, D), dtype=jnp.float32)
        d = jax.random.uniform(k2, (N,), dtype=jnp.float32)
        w = jax.random.uniform(k3, (E,), dtype=jnp.float32)
        gate_w = jax.random.normal(k4, (1, 2 * D), dtype=jnp.float32) * 1.414 * np.sqrt(2.0 / (2 * D + 1))
        gate_b = jnp.zeros((1,), dtype=jnp.float32)
        src = jax.random.randint(k5, (E,), 0, N, dtype=jnp.int64)
        dst = jax.random.randint(k6, (E,), 0, N, dtype=jnp.int64)
        return {'h': h, 'd': d, 'w': w, 'gate_w': gate_w, 'gate_b': gate_b, 'src': src, 'dst': dst}
    _L2_gnn_all = _L2_gnn_setup()
    _L2_gnn_in = {k: v for k, v in _L2_gnn_all.items() if k in ('gate_w', 'gate_b')}
    del _L2_gnn_all

    def _L3_gnn_setup():
        import jax, jax.numpy as jnp
        import numpy as np
        N_NODES = 3125
        N_EDGES = 15625
        D_IN = 128
        D_OUT = 128
        key = jax.random.key(seed)
        k1, k2, k3, k4, k5 = jax.random.split(key, 5)
        feat = jax.random.normal(k1, (N_NODES, D_IN), dtype=jnp.float32)
        edge_src = jax.random.randint(k2, (N_EDGES,), 0, N_NODES, dtype=jnp.int64)
        edge_dst = jax.random.randint(k3, (N_EDGES,), 0, N_NODES, dtype=jnp.int64)
        W = jax.random.normal(k4, (D_OUT, D_IN), dtype=jnp.float32) * (1.0 / np.sqrt(D_IN))
        b = jax.random.normal(k5, (D_OUT,), dtype=jnp.float32) * 0.01
        return {'feat': feat, 'edge_src': edge_src, 'edge_dst': edge_dst, 'W': W, 'b': b}
    _L3_gnn_all = _L3_gnn_setup()
    _L3_gnn_in = {k: v for k, v in _L3_gnn_all.items() if k in ('W', 'b')}
    del _L3_gnn_all
    return {'x': x, 'src': src, 'dst': dst, 'edge_weight': edge_weight, 'L0_gnn_W': _L0_gnn_in['W'], 'L0_gnn_b': _L0_gnn_in['b'], 'L1_gnn_fw1': _L1_gnn_in['fw1'], 'L1_gnn_fb1': _L1_gnn_in['fb1'], 'L1_gnn_fw2': _L1_gnn_in['fw2'], 'L1_gnn_fb2': _L1_gnn_in['fb2'], 'L1_gnn_lin1_w': _L1_gnn_in['lin1_w'], 'L1_gnn_lin2_w': _L1_gnn_in['lin2_w'], 'L1_gnn_lin2_b': _L1_gnn_in['lin2_b'], 'L1_gnn_ln_g': _L1_gnn_in['ln_g'], 'L1_gnn_ln_b': _L1_gnn_in['ln_b'], 'L2_gnn_gate_w': _L2_gnn_in['gate_w'], 'L2_gnn_gate_b': _L2_gnn_in['gate_b'], 'L3_gnn_W': _L3_gnn_in['W'], 'L3_gnn_b': _L3_gnn_in['b']}

def reference(x, src, dst, edge_weight, L0_gnn_W, L0_gnn_b, L1_gnn_fw1, L1_gnn_fb1, L1_gnn_fw2, L1_gnn_fb2, L1_gnn_lin1_w, L1_gnn_lin2_w, L1_gnn_lin2_b, L1_gnn_ln_g, L1_gnn_ln_b, L2_gnn_gate_w, L2_gnn_gate_b, L3_gnn_W, L3_gnn_b):
    import jax
    import jax.numpy as jnp

    def _L0_gnn_ref(x, edge_src, edge_dst, edge_vals, W, b):
        import jax, jax.numpy as jnp
        import numpy as np
        N_NODES = 3125
        N_EDGES = 50000
        D_IN = 128
        D_OUT = 128
        msgs = edge_vals[:, None] * x[edge_src]
        agg = jax.ops.segment_sum(msgs, edge_dst, num_segments=x.shape[0])
        return jnp.einsum('nd,od->no', agg, W) + b

    def _L1_gnn_ref(x, edge_attr, fw1, fb1, fw2, fb2, lin1_w, lin2_w, lin2_b, ln_g, ln_b, edge_index, batch):
        import jax, jax.numpy as jnp
        import numpy as np
        SDIM = 128
        DEPTH = 5
        CUTOFF = 5.0
        NUM_RADIAL = 32
        N_NODES = 50000
        N_EDGES = 12500

        def ssp(v):
            return jax.nn.softplus(v) - jnp.log(2.0).astype(v.dtype)
        src, dst = (edge_index[0], edge_index[1])
        n = x.shape[0]
        offsets = jnp.linspace(0.0, CUTOFF, NUM_RADIAL, dtype=x.dtype)
        coeff = -0.5 / (offsets[1] - offsets[0]) ** 2
        rbf = jnp.exp(coeff * (edge_attr[:, None] - offsets[None, :]) ** 2)
        C = 0.5 * (jnp.cos(jnp.pi * edge_attr / CUTOFF) + 1.0) * (edge_attr < CUTOFF)
        deg = jax.ops.segment_sum(jnp.ones_like(edge_attr), dst, num_segments=n)
        denom = jnp.maximum(deg, 1.0)[:, None]
        for i in range(DEPTH):
            W = ssp(rbf @ fw1[i] + fb1[i]) @ fw2[i] + fb2[i]
            W = W * C[:, None]
            h = x @ lin1_w[i]
            msg = h[src] * W
            agg = jax.ops.segment_sum(msg, dst, num_segments=n) / denom
            x = x + ssp(agg) @ lin2_w[i] + lin2_b[i]
            mu = jnp.mean(x, axis=-1, keepdims=True)
            var = jnp.mean((x - mu) ** 2, axis=-1, keepdims=True)
            x = (x - mu) * jax.lax.rsqrt(var + 1e-05) * ln_g[i] + ln_b[i]
        return x

    def _L2_gnn_ref(h, d, w, gate_w, gate_b, src, dst):
        import jax, jax.numpy as jnp
        import numpy as np
        N, D, E = (3125, 128, 50000)
        w_dst = gate_w[0, :D]
        w_src = gate_w[0, D:]
        s_dst = h @ w_dst
        s_src = h @ w_src
        alpha = jnp.tanh(s_dst[dst] + s_src[src] + gate_b[0])
        e = alpha * d[dst] * d[src] * w
        m = h[src] * e[:, None]
        z = jax.ops.segment_sum(m, dst, num_segments=h.shape[0])
        return z

    def _L3_gnn_ref(feat, edge_src, edge_dst, W, b):
        import jax, jax.numpy as jnp
        import numpy as np
        N_NODES = 3125
        N_EDGES = 15625
        D_IN = 128
        D_OUT = 128
        msgs = feat[edge_src]
        agg = jax.ops.segment_sum(msgs, edge_dst, num_segments=feat.shape[0])
        return agg @ W.T + b
    edge_index = jnp.stack([src, dst])
    deg = jnp.maximum(jax.ops.segment_sum(jnp.ones(dst.shape, jnp.float32), dst, num_segments=3125), 1.0)
    deg_isqrt = deg ** (-0.5)
    batch0 = jnp.zeros((3125,), jnp.int32)
    h = jnp.maximum(_layernorm(x, axis=-1), 0.0)
    x = x + _L0_gnn_ref(h, src, dst, edge_weight, L0_gnn_W, L0_gnn_b)
    h = jnp.maximum(_layernorm(x, axis=-1), 0.0)
    x = x + _L1_gnn_ref(h, edge_weight, L1_gnn_fw1, L1_gnn_fb1, L1_gnn_fw2, L1_gnn_fb2, L1_gnn_lin1_w, L1_gnn_lin2_w, L1_gnn_lin2_b, L1_gnn_ln_g, L1_gnn_ln_b, edge_index, batch0)
    h = jnp.maximum(_layernorm(x, axis=-1), 0.0)
    x = x + _L2_gnn_ref(h, deg_isqrt, edge_weight, L2_gnn_gate_w, L2_gnn_gate_b, src, dst)
    h = jnp.maximum(_layernorm(x, axis=-1), 0.0)
    x = x + _L3_gnn_ref(h, src, dst, L3_gnn_W, L3_gnn_b)
    return x

_drawn_inputs = setup_inputs


def setup_inputs(seed=0):
    import zlib

    import numpy as np

    out = dict(_drawn_inputs(seed))
    spreads = {'L1_gnn_fb1': (0.0, 0.8),
     'L1_gnn_fb2': (0.0, 0.447),
     'L1_gnn_lin2_b': (0.0, 0.287),
     'L1_gnn_ln_g': (1.0, 0.2),
     'L1_gnn_ln_b': (0.0, 0.1)}
    factors = {'L0_gnn_b': 8.0,
     'L1_gnn_fw1': 3.458,
     'L1_gnn_fw2': 3.836,
     'L1_gnn_lin2_w': 3.041,
     'L3_gnn_b': 64.0,
     'L2_gnn_gate_w': 3.372}
    for name, (base, spread) in spreads.items():
        noise = np.random.default_rng([zlib.crc32(name.encode()), seed]).standard_normal(out[name].shape)
        drawn = base * np.exp(spread * noise) if base else spread * noise
        out[name] = jnp.asarray(drawn.astype(out[name].dtype))
    for name, factor in factors.items():
        out[name] = (out[name] * factor).astype(out[name].dtype)
    return out
```

```python
from contextlib import ExitStack
import math

import concourse.bass as bass
from concourse import mybir

F32 = mybir.dt.float32
I32 = mybir.dt.int32
ALU = mybir.AluOpType
ACT = mybir.ActivationFunctionType
AX = mybir.AxisListType.X

P = 128
N_NODES = 3125
N_EDGES = 53125
D = 128
DEPTH = 5
RADIAL = 32
CUTOFF = 5.0
EPS = 1e-5
LN2 = math.log(2.0)

CH = 8
GROUP = CH * P
Q = 4
GROUPS = -(-N_EDGES // GROUP)
TURNS = GROUPS // Q
assert GROUPS == TURNS * Q
LAST = N_EDGES - (GROUPS - 1) * GROUP
LAST_P, LAST_J = LAST // CH, LAST % CH
WIN = 80
TILES = -(-N_NODES // P)
BT = 5
BATCHES = TILES // BT
assert TILES == BATCHES * BT
BN = BT * P
NPAD = TILES * P
TAIL = N_NODES - (TILES - 1) * P
MAX_PASSES = -(-N_NODES // WIN)
NEWTON = 3
ROW2 = D + 4


def take(eng, sem, n=1):
    eng.wait_ge(sem, n)
    eng.sem_inc(sem, -n)


def build(nc, a, out):
    ctx = ExitStack()
    with ctx:
        def sb(name, shape, dt=F32):
            return ctx.enter_context(nc.sbuf_tensor(name, shape, dt))

        def pb(name):
            return ctx.enter_context(nc.psum_tensor(name, [P, 2 * 512], F32))

        def sem(name):
            return ctx.enter_context(nc.semaphore(name))

        table = nc.dram_tensor("table", [NPAD, D], F32, kind="Internal").ap()
        table2 = nc.dram_tensor("table2", [NPAD, ROW2], F32, kind="Internal").ap()

        ident = sb("ident", [P, P])
        ones = sb("ones", [P, P])
        neg_ln2 = sb("neg_ln2", [P, P])
        win_i = sb("win_i", [P, WIN], I32)
        win = sb("win", [P, WIN])
        pass_i = sb("pass_i", [P, MAX_PASSES], I32)
        pass_at = sb("pass_at", [P, MAX_PASSES])
        offset_i = sb("offset_i", [P, 1], I32)
        neg_offset = sb("neg_offset", [P, 1])

        src_i = sb("src_i", [P, (GROUPS + Q) * CH], I32)
        dst_i = sb("dst_i", [P, GROUPS * CH], I32)
        w_e = sb("w_e", [P, GROUPS * CH])
        c_e = sb("c_e", [P, GROUPS * CH])
        dst0 = sb("dst0", [P, GROUPS * CH])
        dst_rel = sb("dst_rel", [P, GROUPS * CH])
        least = sb("least", [GROUPS, 1])
        most = sb("most", [GROUPS, 1])
        least_b = sb("least_b", [GROUPS, P])
        span_b = sb("span_b", [GROUPS, P])
        base0 = sb("base0", [P, GROUPS])
        base_f = sb("base_f", [P, GROUPS])
        base_i = sb("base_i", [P, GROUPS], I32)
        span_max = sb("span_max", [P, 1])
        pass_hit = sb("pass_hit", [P, MAX_PASSES])
        passes_f = sb("passes_f", [P, 1])
        passes_i = sb("passes_i", [P, 1], I32)
        basis = sb("basis", [P, TURNS * GROUP])
        staged_src = sb("staged_src", [P, Q, CH], I32)
        rows = sb("rows", [P, Q, CH, ROW2])
        onehot = sb("onehot", [P, CH, WIN])
        scatter = sb("scatter", [P, CH, WIN])
        gate = sb("gate", [P, CH, WIN])
        slog = sb("slog", [P, 2, 512])
        hidden = sb("hidden", [P, 2, 512])
        filt = sb("filt", [P, 2, 512])
        msg = sb("msg", [P, 2, 512])

        x = sb("x", [P, TILES, D])
        y = sb("y", [P, TILES, D])
        agg = sb("agg", [P, NPAD + WIN])
        deg = sb("deg", [P, NPAD + WIN])
        score = basis[:, 0:NPAD + WIN]
        dcol = sb("dcol", [P, TILES])
        u = sb("u", [P, BN])
        v = sb("v", [P, BN])
        c_t = u[:, 0:GROUPS * CH]
        turns_i = v[:, 0:GROUPS * CH].bitcast(I32)
        dst_row = agg[0:GROUPS, 0:GROUP].bitcast(I32)
        t1 = sb("t1", [P, BT, D])
        x5 = sb("x5", [P, BT, D])
        z5 = sb("z5", [P, BT, D])
        y5 = sb("y5", [P, BT, D])
        yT = sb("yT", [P, BN])
        tab5 = sb("tab5", [P, BT, ROW2])
        stats = sb("stats", [P, BT, 6])
        mv = sb("mv", [P, BT, 2])
        var5 = sb("var5", [P, BT])
        newton = sb("newton", [P, TILES])
        deg_col = sb("deg_col", [P, TILES])
        rstd = sb("rstd", [P, BT, 1])
        nmr = sb("nmr", [P, BT, 1])

        w0 = sb("w0", [P, D])
        w3 = sb("w3", [P, D])
        w0T = sb("w0T", [P, D])
        w3T = sb("w3T", [P, D])
        b0 = sb("b0", [P, D])
        b3 = sb("b3", [P, D])
        fw1 = sb("fw1", [P, DEPTH, D])
        fw1_q = sb("fw1_q", [P, Q, D])
        fb1 = sb("fb1", [P, DEPTH])
        fb1_l = sb("fb1_l", [P, 1])
        nfb1 = sb("nfb1", [P, DEPTH])
        nfb1_l = sb("nfb1_l", [P, 1])
        fb1_ln2 = sb("fb1_ln2", [P, DEPTH, P])
        fw2 = sb("fw2", [P, DEPTH, D])
        fb2 = sb("fb2", [P, DEPTH, D])
        lin1 = sb("lin1", [P, DEPTH + 1, D])
        lin2 = sb("lin2", [P, DEPTH, D])
        lb2 = sb("lb2", [P, DEPTH, D])
        ln_g = sb("ln_g", [P, DEPTH, D])
        ln_b = sb("ln_b", [P, DEPTH, D])
        gate_w = sb("gate_w", [P, 2])
        gate_wb = sb("gate_wb", [P, P])
        gate_b = sb("gate_b", [P, 1])

        pA, pB, pC, pD = pb("pA"), pb("pB"), pb("pC"), pb("pD")

        loaded = sem("loaded")
        pads_set = sem("pads_set")
        pool_own = sem("pool_own")
        consts_made = sem("consts_made")
        dve_own = sem("dve_own")
        act_own = sem("act_own")
        pe_out = sem("pe_out")
        dve_out = sem("dve_out")
        basis_w = sem("basis_w")
        angle_full = sem("angle_full")
        sine_full = sem("sine_full")
        basis_made = sem("basis_made")
        gathers = [sem(f"gathers{q}") for q in range(Q)]
        gathered = [sem(f"gathered{q}") for q in range(Q)]
        staged = [sem(f"staged{q}") for q in range(Q)]
        table_dma = sem("table_dma")
        table_ready = sem("table_ready")
        scatter_full = sem("scatter_full")
        sum_full = sem("sum_full")
        sum_free = sem("sum_free")
        gate_in = sem("gate_in")
        gate_full = sem("gate_full")
        filter_ready = sem("filter_ready")
        bias_ready = sem("bias_ready")
        deg_full = sem("deg_full")
        col_full = sem("col_full")
        hid_full = [sem(f"hid_full{h}") for h in range(2)]
        slog_full = [sem(f"slog_full{h}") for h in range(2)]
        u_log_full = sem("u_log_full")
        ssp_full = [sem(f"ssp_full{h}") for h in range(2)]
        filt_full = [sem(f"filt_full{h}") for h in range(2)]
        msg_full = [sem(f"msg_full{h}") for h in range(2)]
        agg_full = sem("agg_full")
        v_full = sem("v_full")
        lin_full = sem("lin_full")
        ln_full = sem("ln_full")
        norm_full = sem("norm_full")
        y_full = sem("y_full")
        yT_ps = sem("yT_ps")
        yT_full = sem("yT_full")
        tab_ps = sem("tab_ps")
        tab_full = sem("tab_full")
        batch_done = sem("batch_done")
        x_done = sem("x_done")
        stored = sem("stored")

        def per_chunk(tile, at):
            return tile[:, bass.ds(at, CH)].unsqueeze(2).broadcast_to([P, CH, WIN])

        def over_chunks(row):
            return row.unsqueeze(1).broadcast_to([P, CH, WIN])

        def over_tiles(row):
            return row.unsqueeze(1).broadcast_to([P, BT, D])

        def per_tile(cols):
            return cols.broadcast_to([P, BT, D])

        with nc.Block() as block:
            n_loads = 0

            @block.sync
            def _(sp):
                def load(dst, src, turned=False):
                    sp.dma_start(dst, src, allow_slow_non_contiguous=turned).then_inc(loaded, 16)

                def edges(dst, src):
                    full = (GROUPS - 1) * GROUP
                    load(dst[:, 0:(GROUPS - 1) * CH].rearrange("p (g j) -> p g j", j=CH),
                         src[0:full].rearrange("(g p j) -> p g j", p=P, j=CH))
                    load(dst[0:LAST_P, (GROUPS - 1) * CH:GROUPS * CH],
                         src[full:full + LAST_P * CH].rearrange("(p j) -> p j", j=CH))
                    load(dst[LAST_P:LAST_P + 1, (GROUPS - 1) * CH:(GROUPS - 1) * CH + LAST_J],
                         src[full + LAST_P * CH:N_EDGES].rearrange("(a j) -> a j", a=1))

                full = (GROUPS - 1) * GROUP
                load(dst_row[0:GROUPS - 1, :], a["dst"][0:full].rearrange("(g e) -> g e", e=GROUP))
                load(dst_row[GROUPS - 1:GROUPS, 0:LAST], a["dst"][full:N_EDGES].rearrange("(a e) -> a e", a=1))
                load(dst_row[GROUPS - 1:GROUPS, LAST:GROUP],
                     a["dst"][N_EDGES - (GROUP - LAST):N_EDGES].rearrange("(a e) -> a e", a=1))
                sp.wait_ge(pads_set, 1)
                edges(dst_i, a["dst"])
                edges(src_i, a["src"])
                edges(w_e, a["edge_weight"])
                load(src_i[:, GROUPS * CH:(GROUPS + Q) * CH].rearrange("p (g j) -> p g j", j=CH),
                     a["src"][0:Q * GROUP].rearrange("(g p j) -> p g j", p=P, j=CH))
                load(x[:, 0:TILES - 1, :], a["x"][0:(TILES - 1) * P, :].rearrange("(t p) d -> p t d", p=P))
                load(x[0:TAIL, TILES - 1, :], a["x"][(TILES - 1) * P:N_NODES, :])
                load(w0[:, :], a["L0_gnn_W"])
                load(w3[:, :], a["L3_gnn_W"])
                load(b0[:, :], a["L0_gnn_b"].partition_broadcast(P))
                load(b3[:, :], a["L3_gnn_b"].partition_broadcast(P))
                for q in range(Q):
                    load(fw1[q * RADIAL:(q + 1) * RADIAL, :, :], a["L1_gnn_fw1"].rearrange("l r d -> r l d"))
                load(fb1[:, :], a["L1_gnn_fb1"].rearrange("l d -> d l"), turned=True)
                load(fw2[:, :, :], a["L1_gnn_fw2"].rearrange("l k d -> k l d"))
                load(lin1[:, 0:DEPTH, :], a["L1_gnn_lin1_w"].rearrange("l k d -> k l d"))
                load(lin2[:, :, :], a["L1_gnn_lin2_w"].rearrange("l k d -> k l d"))
                for dst, src in ((fb2, "fb2"), (lb2, "lin2_b"), (ln_g, "ln_g"), (ln_b, "ln_b")):
                    load(dst[:, :, :], a["L1_gnn_" + src].partition_broadcast(P))
                load(gate_w[:, :], a["L2_gnn_gate_w"].rearrange("a (s d) -> d (a s)", d=D), turned=True)
                load(gate_b[:, :], a["L2_gnn_gate_b"].partition_broadcast(P))

            N_LOADS = 3 + 9 + 1 + 2 + 4 + Q + 4 + 4 + 2

            @block.scalar
            def _(act):
                act.wait_ge(pads_set, 2)
                for q in range(Q):
                    n = TURNS if q < Q - 1 else TURNS - 1
                    act.dma_start(
                        basis[q * RADIAL:(q + 1) * RADIAL, 0:n * GROUP].rearrange("r (i e) -> r i e", e=GROUP),
                        a["edge_weight"][0:(GROUPS - 1) * GROUP]
                        .rearrange("(i s e) -> i s e", s=1, e=GROUP)[q:(n - 1) * Q + q + 1:Q, 0, :]
                        .partition_broadcast(RADIAL)).then_inc(basis_w, 16)
                act.dma_start(basis[(Q - 1) * RADIAL:P, (TURNS - 1) * GROUP:(TURNS - 1) * GROUP + LAST],
                              a["edge_weight"][(GROUPS - 1) * GROUP:N_EDGES].partition_broadcast(RADIAL))\
                   .then_inc(basis_w, 16)
                act.wait_ge(angle_full, 1)
                act.activation(c_t[:, :], c_e[:, :], ACT.Sin, scale=math.pi / (2 * CUTOFF)).then_inc(sine_full, 1)
                act.wait_ge(basis_w, 16 * (Q + 1))
                act.wait_ge(consts_made, 2)
                act.activation(basis[:, :], basis[:, :], ACT.Square, bias=neg_offset[:, 0:1]).then_inc(act_own, 1)
                take(act, act_own)
                step = CUTOFF / (RADIAL - 1)
                act.activation(basis[:, :], basis[:, :], ACT.Exp, scale=-0.5 / (step * step))\
                   .then_inc(basis_made, 1)

            @block.gpsimd
            def _(pool):
                pool.memset(ident[:, :], 0.0).then_inc(pool_own, 1)
                pool.iota(win_i[:, :], pattern=[[1, WIN]], base=0, channel_multiplier=0)
                pool.iota(pass_i[:, :], pattern=[[WIN, MAX_PASSES]], base=0, channel_multiplier=0)
                pool.iota(offset_i[:, :], pattern=[[0, 1]], base=0, channel_multiplier=1)
                take(pool, pool_own)
                pool.affine_select(out=ident[:, :], in_=ident[:, :], compare_op=ALU.not_equal, fill=1.0,
                                   base=0, pattern=[[-1, P]], channel_multiplier=1).then_inc(consts_made, 1)

            @block.tensor
            def _(pe):
                pe.wait_ge(dve_out, 1)
                pe.wait_ge(consts_made, 1)
                pe.matmul(pA[:, 0:GROUPS], least_b[:, :], ident[0:GROUPS, 0:GROUPS], start=True, stop=True)
                pe.matmul(pB[:, 0:GROUPS], span_b[:, :], ident[0:GROUPS, 0:GROUPS], start=True, stop=True)\
                  .then_inc(pe_out, 1)
                pe.wait_ge(loaded, 16 * N_LOADS)
                pe.transpose(pC[:, 0:P], w0[:, :], ident[:, :])
                pe.transpose(pD[:, 0:P], w3[:, :], ident[:, :]).then_inc(pe_out, 1)
                pe.wait_ge(dve_out, 2)
                for l in range(DEPTH):
                    pe.matmul(pA[:, l * D:(l + 1) * D], fb1_ln2[:, l, :], fw2[:, l, :], start=True, stop=True)
                    last = pe.matmul(pB[:, l * D:(l + 1) * D], neg_ln2[:, :], lin2[:, l, :], start=True, stop=True)
                last.then_inc(pe_out, 1)

            @block.vector
            def _(dve):
                def own(ins):
                    ins.then_inc(dve_own, 1)
                    take(dve, dve_own)

                dve.memset(src_i[:, :], 0)
                dve.memset(dst_i[:, :], -1)
                dve.memset(w_e[:, :], 0.0)
                dve.memset(x[:, TILES - 1, :], 0.0).then_inc(pads_set, 1)
                dve.memset(basis[(Q - 1) * RADIAL:P, (TURNS - 1) * GROUP + LAST:TURNS * GROUP], 0.0)\
                   .then_inc(pads_set, 1)
                dve.memset(neg_ln2[:, :], -LN2)
                dve.memset(lin1[:, DEPTH, :], 0.0)
                dve.memset(fw1_q[:, :, :], 0.0)
                dve.memset(tab5[:, :, :], 0.0)
                dve.memset(deg[:, :], 0.0)
                own(dve.memset(ones[:, :], 1.0))
                dve.wait_ge(consts_made, 1)
                dve.tensor_copy(win[:, :], win_i[:, :])
                dve.tensor_copy(pass_at[:, :], pass_i[:, :])
                own(dve.tensor_scalar(offset_i[:, :], offset_i[:, :], RADIAL - 1, None, ALU.bitwise_and))
                dve.tensor_scalar(neg_offset[:, :], offset_i[:, :], -CUTOFF / (RADIAL - 1), None, ALU.mult)\
                   .then_inc(consts_made, 1)
                dve.wait_ge(loaded, 16 * N_LOADS)
                dve.tensor_reduce(least[:, :], dst_row[:, :], AX, ALU.min)
                own(dve.tensor_reduce(most[:, :], dst_row[:, :], AX, ALU.max))
                own(dve.tensor_tensor(most[:, :], most[:, :], least[:, :], ALU.subtract))
                dve.tensor_copy(least_b[:, :], least[:, 0:1].broadcast_to([GROUPS, P]))
                dve.tensor_copy(span_b[:, :], most[:, 0:1].broadcast_to([GROUPS, P])).then_inc(dve_out, 1)
                own(dve.tensor_scalar(turns_i[:, :], w_e[:, :], 1.0 / (2 * CUTOFF), None, ALU.mult))
                dve.scalar_tensor_tensor(c_e[:, :], turns_i[:, :], -2 * CUTOFF, w_e[:, :], ALU.mult, ALU.add)\
                   .then_inc(angle_full, 1)
                dve.wait_ge(pe_out, 1)
                dve.tensor_copy(base0[:, :], pA[:, 0:GROUPS])
                own(dve.tensor_reduce(span_max[:, :], pB[:, 0:GROUPS], AX, ALU.max))
                own(dve.tensor_scalar(pass_hit[:, :], pass_at[:, :], span_max[:, 0:1], None, ALU.is_le))
                own(dve.tensor_reduce(passes_f[:, :], pass_hit[:, :], AX, ALU.add))
                dve.tensor_copy(passes_i[:, :], passes_f[:, :])
                own(dve.tensor_copy(dst0[:, :], dst_i[:, :]))
                dst0_g = dst0[:, :].rearrange("p (g j) -> p g j", j=CH)
                own(dve.tensor_tensor(dst0_g, dst0_g, base0[:, :].unsqueeze(2).broadcast_to([P, GROUPS, CH]),
                                      ALU.subtract))
                dve.wait_ge(pe_out, 2)
                dve.tensor_copy(w0T[:, :], pC[:, 0:P])
                dve.tensor_copy(w3T[:, :], pD[:, 0:P])
                dve.tensor_scalar(nfb1[:, :], fb1[:, :], -1.0, None, ALU.mult)
                dve.tensor_scalar(fb1_ln2[:, :, :], fb1[:, :].unsqueeze(2).broadcast_to([P, DEPTH, P]), -LN2, None,
                                  ALU.add).then_inc(dve_out, 1)
                dve.wait_ge(sine_full, 1)
                own(dve.tensor_tensor(c_t[:, :], c_t[:, :], c_t[:, :], ALU.mult))
                own(dve.tensor_scalar(c_t[:, :], c_t[:, :], -1.0, 1.0, ALU.mult, ALU.add))
                own(dve.tensor_scalar(c_e[:, :], w_e[:, :], CUTOFF, None, ALU.is_lt))
                dve.tensor_tensor(c_e[:, :], c_e[:, :], c_t[:, :], ALU.mult)
                for q in range(Q):
                    dve.tensor_copy(staged_src[:, q, :], src_i[:, q * CH:(q + 1) * CH])
                dve.tensor_copy(gate_wb[:, :], gate_w[:, 0:1].broadcast_to([P, P]))
                dve.wait_ge(pe_out, 3)
                for bias, ps in ((fb2, pA), (lb2, pB)):
                    flat = bias[:, :, :].rearrange("p l d -> p (l d)")
                    dve.tensor_tensor(flat, flat, ps[:, 0:DEPTH * D], ALU.add)

        with nc.Block() as block:

            @block.sync
            def _(sp):
                n_pass = sp.value_load(passes_i[0:1, 0:1], min_val=1, max_val=MAX_PASSES)
                with sp.Fori(0, n_pass * ((DEPTH + 3) * TURNS)) as n:
                    for q in range(Q):
                        sp.wait_ge(gathers[q], n * (CH * 16) + CH * 16)
                        sp.sem_inc(gathered[q], 1)
                take(sp, x_done)
                sp.dma_start(out[0:(TILES - 1) * P, :].rearrange("(t p) d -> p t d", p=P),
                             x[:, 0:TILES - 1, :]).then_inc(stored, 16)
                sp.dma_start(out[(TILES - 1) * P:N_NODES, :], x[0:TAIL, TILES - 1, :]).then_inc(stored, 16)
                sp.wait_ge(stored, 32)

            @block.gpsimd
            def _(pool):
                n_pass = pool.value_load(passes_i[0:1, 0:1], min_val=1, max_val=MAX_PASSES)

                def gather(tab, width):
                    take(pool, table_ready)
                    with pool.Fori(0, n_pass):
                        with pool.Fori(0, TURNS):
                            for q in range(Q):
                                take(pool, staged[q])
                                for j in range(CH):
                                    pool.indirect_dma_start(
                                        out=rows[:, q, j, 0:width], out_offset=None, in_=tab[:, :],
                                        in_offset=bass.IndirectOffsetOnAxis(ap=staged_src[:, q, j:j + 1], axis=0),
                                    ).then_inc(gathers[q], 16)

                gather(table, D)
                with pool.Fori(0, DEPTH):
                    gather(table, D)
                take(pool, table_ready)
                gather(table2, ROW2)
                gather(table, D)

            @block.tensor
            def _(pe):
                n_pass = pe.value_load(passes_i[0:1, 0:1], min_val=1, max_val=MAX_PASSES)

                def scatter_rows(q, degrees):
                    take(pe, scatter_full)
                    take(pe, sum_free)
                    if degrees:
                        for j in range(CH):
                            pe.matmul(pD[:, 0:WIN], ones[:, :], onehot[:, j, :], start=(j == 0), stop=(j == CH - 1))
                    for j in range(CH):
                        mm = pe.matmul(pC[:, 0:WIN], rows[:, q, j, 0:D], scatter[:, j, :],
                                       start=(j == 0), stop=(j == CH - 1))
                    mm.then_inc(sum_full, 1)

                def plain_edges(degrees=False):
                    with pe.Fori(0, n_pass):
                        with pe.Fori(0, TURNS):
                            for q in range(Q):
                                scatter_rows(q, degrees)

                def conv_edges(l):
                    take(pe, filter_ready)
                    with pe.Fori(0, n_pass):
                        with pe.Fori(0, TURNS) as i:
                            for q in range(Q):
                                for h in range(2):
                                    pe.matmul(pA[:, h * 512:(h + 1) * 512], fw1_q[:, q, :],
                                              basis[:, bass.ds(i * GROUP + h, 512, 2)],
                                              start=True, stop=True).then_inc(hid_full[h], 1)
                                for h in range(2):
                                    take(pe, ssp_full[h])
                                    for c in range(CH // 2):
                                        mm = pe.matmul(pB[:, h * 512 + c * D:h * 512 + (c + 1) * D],
                                                       hidden[:, h, c:512:CH // 2], fw2[:, l, :],
                                                       start=True, stop=True)
                                    mm.then_inc(filt_full[h], 1)
                                take(pe, scatter_full)
                                take(pe, sum_free)
                                for h in range(2):
                                    take(pe, msg_full[h])
                                    for c in range(CH // 2):
                                        mm = pe.matmul(pC[:, 0:WIN], msg[:, h, c * D:(c + 1) * D],
                                                       scatter[:, 2 * c + h, :],
                                                       start=(h == 0 and c == 0), stop=(h == 1 and c == CH // 2 - 1))
                                mm.then_inc(sum_full, 1)

                def linear(weights):
                    take(pe, v_full)
                    for k in range(BT):
                        mm = pe.matmul(pA[:, k * D:(k + 1) * D], v[:, k * P:(k + 1) * P], weights, start=True, stop=True)
                    mm.then_inc(lin_full, 1)

                def turn():
                    take(pe, y_full)
                    for k in range(BT):
                        mm = pe.transpose(pB[:, k * P:(k + 1) * P], y5[:, k, :], ident[:, :])
                    mm.then_inc(yT_ps, 1)

                def table_rows(weights):
                    take(pe, yT_full)
                    for k in range(BT):
                        mm = pe.matmul(pC[:, k * D:(k + 1) * D], yT[:, k * P:(k + 1) * P], weights, start=True, stop=True)
                    mm.then_inc(tab_ps, 1)

                plain_edges(degrees=True)
                take(pe, deg_full)
                for t in range(TILES):
                    mm = pe.matmul(pD[:, t:t + 1], deg[0:1, t * P:(t + 1) * P], ones[0:1, 0:1], start=True, stop=True)
                mm.then_inc(lin_full, 1)
                with pe.Fori(0, BATCHES):
                    linear(w0T[:, :])
                    turn()
                    table_rows(lin1[:, 0, :])
                with pe.Fori(0, DEPTH) as l:
                    conv_edges(l)
                    with pe.Fori(0, BATCHES):
                        linear(lin2[:, l, :])
                        turn()
                        table_rows(lin1[:, l + 1, :])
                with pe.Fori(0, BATCHES):
                    turn()
                    take(pe, yT_full)
                    pe.matmul(pA[:, 0:512], gate_wb[:, :], yT[:, 0:512], start=True, stop=True)
                    pe.matmul(pA[:, 512:BN], gate_wb[:, :], yT[:, 512:BN], start=True, stop=True).then_inc(tab_ps, 1)
                    for k in range(BT):
                        mm = pe.matmul(pC[:, k:k + 1], yT[:, k * P:(k + 1) * P], gate_w[:, 1:2], start=True, stop=True)
                    mm.then_inc(col_full, 1)
                plain_edges()
                with pe.Fori(0, BATCHES):
                    take(pe, v_full)
                    for k in range(BT):
                        mm = pe.transpose(pA[:, k * D:(k + 1) * D], v[:, k * P:(k + 1) * P], ident[:, :])
                    mm.then_inc(lin_full, 1)
                plain_edges()
                with pe.Fori(0, BATCHES):
                    linear(w3T[:, :])

            @block.scalar
            def _(act):
                n_pass = act.value_load(passes_i[0:1, 0:1], min_val=1, max_val=MAX_PASSES)

                def own(ins):
                    ins.then_inc(act_own, 1)
                    take(act, act_own)

                def softplus_log(dst, arg, full, **bias):
                    own(act.activation(dst, arg, ACT.Abs, **bias))
                    own(act.activation(dst, dst, ACT.Exp, scale=-1.0))
                    act.activation(dst, dst, ACT.Ln, bias=1.0).then_inc(full, 1)

                def write_table(tab, width, at):
                    for k in range(BT):
                        act.dma_start(tab[bass.ds(at + k * P, P), 0:width], tab5[:, k, 0:width]).then_inc(table_dma, 16)
                    take(act, table_dma, 16 * BT)

                def take_sums(at):
                    act.activation(v[:, :], agg[:, bass.ds(at, BN)], ACT.Copy).then_inc(v_full, 1)

                def normalise(func):
                    take(act, ln_full)
                    for k in range(BT):
                        ins = act.activation(z5[:, k, :], x5[:, k, :], func, bias=nmr[:, k, :], scale=rstd[:, k, :])
                    ins.then_inc(norm_full, 1)

                def turned():
                    take(act, yT_ps)
                    act.activation(yT[:, :], pB[:, 0:BN], ACT.Copy).then_inc(yT_full, 1)

                def rows_out(at):
                    take(act, tab_ps)
                    own(act.activation(tab5[:, :, 0:D], pC[:, 0:BN].rearrange("p (k d) -> p k d", d=D), ACT.Copy))
                    write_table(table, D, at)
                    act.sem_inc(batch_done, 1)

                with act.Fori(0, BATCHES) as b:
                    take(act, ln_full)
                    for k in range(BT):
                        ins = act.activation(tab5[:, k, 0:D], x5[:, k, :], ACT.Relu, bias=nmr[:, k, :], scale=rstd[:, k, :])
                    own(ins)
                    write_table(table, D, b * BN)
                    act.sem_inc(batch_done, 1)
                act.sem_inc(table_ready, 1)
                take(act, agg_full)
                with act.Fori(0, BATCHES) as b:
                    take_sums(b * BN)
                    normalise(ACT.Relu)
                    turned()
                    rows_out(b * BN)
                act.sem_inc(table_ready, 1)
                with act.Fori(0, DEPTH):
                    take(act, bias_ready)
                    with act.Fori(0, n_pass):
                        with act.Fori(0, TURNS):
                            for q in range(Q):
                                for h in range(2):
                                    take(act, hid_full[h])
                                    softplus_log(slog[:, h, :], pA[:, h * 512:(h + 1) * 512], slog_full[h],
                                                 bias=fb1_l[:, 0:1])
                    with act.Fori(0, BATCHES) as b:
                        take(act, agg_full)
                        softplus_log(yT[:, :], u[:, :], u_log_full)
                        normalise(ACT.Identity)
                        turned()
                        rows_out(b * BN)
                    act.sem_inc(table_ready, 1)
                with act.Fori(0, BATCHES) as b:
                    normalise(ACT.Relu)
                    turned()
                    take(act, tab_ps)
                    own(act.activation(score[:, bass.ds(b * BN, BN)], pA[:, 0:BN], ACT.Copy))
                    take(act, tab_full)
                    write_table(table2, ROW2, b * BN)
                    act.sem_inc(batch_done, 1)
                act.sem_inc(table_ready, 1)
                with act.Fori(0, n_pass):
                    with act.Fori(0, TURNS):
                        for q in range(Q):
                            take(act, gate_in)
                            act.activation(gate[:, :, :], gate[:, :, :], ACT.Tanh).then_inc(gate_full, 1)
                take(act, agg_full)
                with act.Fori(0, BATCHES) as b:
                    take_sums(b * BN)
                    take(act, ln_full)
                    for k in range(BT):
                        ins = act.activation(tab5[:, k, 0:D], x5[:, k, :], ACT.Relu, bias=nmr[:, k, :], scale=rstd[:, k, :])
                    own(ins)
                    write_table(table, D, b * BN)
                    act.sem_inc(batch_done, 1)
                act.sem_inc(table_ready, 1)
                take(act, agg_full)
                with act.Fori(0, BATCHES) as b:
                    take_sums(b * BN)
                    take(act, ln_full)

            @block.vector
            def _(dve):
                n_pass = dve.value_load(passes_i[0:1, 0:1], min_val=1, max_val=MAX_PASSES)

                def own(ins):
                    ins.then_inc(dve_own, 1)
                    take(dve, dve_own)

                for q in range(Q):
                    dve.sem_inc(staged[q], 1)
                dve.sem_inc(sum_free, 1)

                def start_sums():
                    dve.memset(agg[:, :], 0.0)
                    dve.tensor_copy(dst_rel[:, :], dst0[:, :])
                    dve.tensor_copy(base_f[:, :], base0[:, :])
                    own(dve.tensor_copy(base_i[:, :], base0[:, :]))

                def next_pass():
                    dve.tensor_scalar(dst_rel[:, :], dst_rel[:, :], -float(WIN), None, ALU.add)
                    own(dve.tensor_scalar(base_f[:, :], base_f[:, :], float(WIN), float(NPAD), ALU.add, ALU.min))
                    own(dve.tensor_copy(base_i[:, :], base_f[:, :]))

                def window_start(i, q):
                    return dve.value_load(base_i[0:1, bass.ds(i * Q + q, 1)], min_val=0, max_val=NPAD)

                def match(dst, i, q):
                    own(dve.tensor_tensor(dst[:, :, :], over_chunks(win[:, :]), per_chunk(dst_rel, i * (Q * CH) + q * CH),
                                          ALU.is_equal))

                def add_sums(i, q, base, degrees=False):
                    take(dve, sum_full)
                    dve.tensor_copy(staged_src[:, q, :], src_i[:, bass.ds(i * (Q * CH) + (Q + q) * CH, CH)])\
                       .then_inc(staged[q], 1)
                    if degrees:
                        own(dve.tensor_tensor(deg[:, bass.ds(base, WIN)], deg[:, bass.ds(base, WIN)], pD[:, 0:WIN], ALU.add))
                    dve.tensor_tensor(agg[:, bass.ds(base, WIN)], agg[:, bass.ds(base, WIN)], pC[:, 0:WIN], ALU.add)\
                       .then_inc(sum_free, 1)

                def last_sum():
                    dve.wait_ge(sum_free, 1)

                def plain_edges(kind):
                    start_sums()
                    with dve.Fori(0, n_pass):
                        with dve.Fori(0, TURNS) as i:
                            for q in range(Q):
                                take(dve, gathered[q])
                                base = window_start(i, q)
                                at = i * (Q * CH) + q * CH
                                if kind == "count":
                                    dve.tensor_tensor(scatter[:, :, :], over_chunks(win[:, :]), per_chunk(dst_rel, at),
                                                      ALU.is_equal).then_inc(scatter_full, 1)
                                elif kind == "weight":
                                    match(onehot, i, q)
                                    dve.tensor_tensor(scatter[:, :, :], onehot[:, :, :], per_chunk(w_e, at), ALU.mult)\
                                       .then_inc(scatter_full, 1)
                                else:
                                    dve.tensor_tensor(gate[:, :, :], over_chunks(score[:, bass.ds(base, WIN)]),
                                                      rows[:, q, :, D:D + 1].broadcast_to([P, CH, WIN]), ALU.add)\
                                       .then_inc(gate_in, 1)
                                    match(onehot, i, q)
                                    own(dve.tensor_tensor(onehot[:, :, :], onehot[:, :, :], per_chunk(w_e, at), ALU.mult))
                                    take(dve, gate_full)
                                    dve.tensor_tensor(scatter[:, :, :], onehot[:, :, :], gate[:, :, :], ALU.mult)\
                                       .then_inc(scatter_full, 1)
                                add_sums(i, q, base, degrees=(kind == "weight"))
                        next_pass()
                    last_sum()

                def conv_edges(l):
                    start_sums()
                    for q in range(Q):
                        dve.tensor_copy(fw1_q[q * RADIAL:(q + 1) * RADIAL, q, :], fw1[q * RADIAL:(q + 1) * RADIAL, l, :])
                    dve.tensor_copy(nfb1_l[:, :], nfb1[:, bass.ds(l, 1)]).then_inc(filter_ready, 1)
                    own(dve.tensor_copy(fb1_l[:, :], fb1[:, bass.ds(l, 1)]))
                    dve.sem_inc(bias_ready, 1)
                    with dve.Fori(0, n_pass):
                        with dve.Fori(0, TURNS) as i:
                            for q in range(Q):
                                base = window_start(i, q)
                                match(onehot, i, q)
                                dve.tensor_tensor(scatter[:, :, :], onehot[:, :, :],
                                                  per_chunk(c_e, i * (Q * CH) + q * CH), ALU.mult)\
                                   .then_inc(scatter_full, 1)
                                for h in range(2):
                                    take(dve, slog_full[h])
                                    dve.scalar_tensor_tensor(hidden[:, h, :], pA[:, h * 512:(h + 1) * 512],
                                                             nfb1_l[:, 0:1], slog[:, h, :], ALU.max, ALU.add)\
                                       .then_inc(ssp_full[h], 1)
                                for h in range(2):
                                    take(dve, filt_full[h])
                                    f4 = filt[:, h, :].rearrange("p (c d) -> p c d", d=D)
                                    own(dve.tensor_tensor(
                                        f4, pB[:, h * 512:(h + 1) * 512].rearrange("p (c d) -> p c d", d=D),
                                        fb2[:, l, :].unsqueeze(1).broadcast_to([P, CH // 2, D]), ALU.add))
                                    if h == 0:
                                        take(dve, gathered[q])
                                    dve.tensor_tensor(msg[:, h, :].rearrange("p (c d) -> p c d", d=D), f4,
                                                      rows[:, q, h:CH:2, 0:D], ALU.mult).then_inc(msg_full[h], 1)
                                add_sums(i, q, base)
                        next_pass()
                    last_sum()

                def rsqrt(root, arg, tmp):
                    own(dve.tensor_scalar(tmp.bitcast(I32), arg.bitcast(I32), 1, None, ALU.logical_shift_right))
                    own(dve.tensor_scalar(root.bitcast(I32), tmp.bitcast(I32), -1.0, float(0x5F3759DF), ALU.mult, ALU.add))
                    for _ in range(NEWTON):
                        own(dve.scalar_tensor_tensor(tmp, root, -0.5, root, ALU.mult, ALU.mult))
                        own(dve.tensor_tensor(tmp, tmp, arg, ALU.mult))
                        own(dve.scalar_tensor_tensor(root, tmp, 1.5, root, ALU.add, ALU.mult))

                def statistics():
                    for k in range(BT):
                        ins = dve.bn_stats(stats[:, k, :], x5[:, k, :])
                    own(ins)
                    for k in range(BT):
                        ins = dve.bn_aggr(mv[:, k, :], stats[:, k, :])
                    own(ins)
                    own(dve.tensor_scalar(var5[:, :], mv[:, :, 1], EPS, None, ALU.add))
                    rsqrt(rstd[:, :, 0], var5[:, :], newton[:, 0:BT])
                    dve.scalar_tensor_tensor(nmr[:, :, :], mv[:, :, 0:1], -1.0, rstd[:, :, :], ALU.mult, ALU.mult)\
                       .then_inc(ln_full, 1)

                def tiles(tile, b):
                    return tile[:, bass.ds(b * BT, BT), :]

                psum_tiles = pA[:, 0:BN].rearrange("p (k d) -> p k d", d=D)

                with dve.Fori(0, BATCHES) as b:
                    own(dve.tensor_copy(x5[:, :, :], tiles(x, b)))
                    statistics()
                    take(dve, batch_done)

                plain_edges("weight")
                dve.sem_inc(agg_full, 1)
                dve.sem_inc(deg_full, 1)
                take(dve, lin_full)
                own(dve.tensor_scalar(deg_col[:, :], pD[:, 0:TILES], 1.0, None, ALU.max))
                rsqrt(dcol[:, :], deg_col[:, :], newton[:, 0:TILES])
                own(dve.tensor_scalar(deg[:, :], deg[:, :], 1.0, None, ALU.max))
                own(dve.reciprocal(deg[:, :], deg[:, :]))
                with dve.Fori(0, BATCHES) as b:
                    take(dve, lin_full)
                    own(dve.tensor_tensor(t1[:, :, :], psum_tiles, over_tiles(b0[:, :]), ALU.add))
                    own(dve.tensor_tensor(x5[:, :, :], t1[:, :, :], tiles(x, b), ALU.add))
                    dve.tensor_copy(tiles(x, b), x5[:, :, :])
                    statistics()
                    take(dve, norm_full)
                    dve.tensor_copy(tiles(y, b), z5[:, :, :])
                    dve.tensor_copy(y5[:, :, :], z5[:, :, :]).then_inc(y_full, 1)
                    take(dve, batch_done)

                with dve.Fori(0, DEPTH) as l:
                    conv_edges(l)
                    with dve.Fori(0, BATCHES) as b:
                        dve.tensor_tensor(u[:, :], agg[:, bass.ds(b * BN, BN)], deg[:, bass.ds(b * BN, BN)], ALU.mult)\
                           .then_inc(agg_full, 1)
                        take(dve, u_log_full)
                        dve.scalar_tensor_tensor(v[:, :], u[:, :], 0.0, yT[:, :], ALU.max, ALU.add).then_inc(v_full, 1)
                        take(dve, lin_full)
                        own(dve.tensor_tensor(t1[:, :, :], psum_tiles, over_tiles(lb2[:, l, :]), ALU.add))
                        own(dve.tensor_tensor(x5[:, :, :], t1[:, :, :], tiles(y, b), ALU.add))
                        statistics()
                        take(dve, norm_full)
                        own(dve.tensor_tensor(t1[:, :, :], z5[:, :, :], over_tiles(ln_g[:, l, :]), ALU.mult))
                        own(dve.tensor_tensor(y5[:, :, :], t1[:, :, :], over_tiles(ln_b[:, l, :]), ALU.add))
                        dve.tensor_copy(tiles(y, b), y5[:, :, :]).then_inc(y_full, 1)
                        take(dve, batch_done)

                own(dve.memset(score[:, NPAD:NPAD + WIN], 0.0))
                with dve.Fori(0, BATCHES) as b:
                    own(dve.tensor_tensor(x5[:, :, :], tiles(x, b), tiles(y, b), ALU.add))
                    dve.tensor_copy(tiles(x, b), x5[:, :, :])
                    statistics()
                    take(dve, norm_full)
                    dve.tensor_copy(y5[:, :, :], z5[:, :, :]).then_inc(y_full, 1)
                    dve.tensor_tensor(tab5[:, :, 0:D], z5[:, :, :],
                                      per_tile(dcol[:, bass.ds(b * BT, BT)].unsqueeze(2)), ALU.mult)
                    take(dve, col_full)
                    dve.tensor_scalar(tab5[:, :, D:D + 1], pC[:, 0:BT].unsqueeze(2), gate_b[:, 0:1], None, ALU.add)\
                       .then_inc(tab_full, 1)
                    take(dve, batch_done)
                plain_edges("gate")
                dve.sem_inc(agg_full, 1)
                with dve.Fori(0, BATCHES) as b:
                    take(dve, lin_full)
                    own(dve.tensor_tensor(t1[:, :, :], psum_tiles,
                                          per_tile(dcol[:, bass.ds(b * BT, BT)].unsqueeze(2)), ALU.mult))
                    own(dve.tensor_tensor(x5[:, :, :], t1[:, :, :], tiles(x, b), ALU.add))
                    dve.tensor_copy(tiles(x, b), x5[:, :, :])
                    statistics()
                    take(dve, batch_done)

                plain_edges("count")
                dve.sem_inc(agg_full, 1)
                with dve.Fori(0, BATCHES) as b:
                    take(dve, lin_full)
                    own(dve.tensor_tensor(t1[:, :, :], psum_tiles, over_tiles(b3[:, :]), ALU.add))
                    own(dve.tensor_tensor(tiles(x, b), t1[:, :, :], tiles(x, b), ALU.add))
                    dve.sem_inc(ln_full, 1)
                dve.sem_inc(x_done, 1)


_INS = ['x', 'src', 'dst', 'edge_weight', 'L0_gnn_W', 'L0_gnn_b', 'L1_gnn_fw1', 'L1_gnn_fb1', 'L1_gnn_fw2',
        'L1_gnn_fb2', 'L1_gnn_lin1_w', 'L1_gnn_lin2_w', 'L1_gnn_lin2_b', 'L1_gnn_ln_g', 'L1_gnn_ln_b',
        'L2_gnn_gate_w', 'L2_gnn_gate_b', 'L3_gnn_W', 'L3_gnn_b']


def kernel(**inputs):
    import numpy as np
    import concourse.bacc as bacc
    from concourse.bass_utils import run_bass_kernel_spmd as run

    nc = bacc.Bacc("TRN2", target_bir_lowering=False, num_devices=1)
    arrays, args = {}, {}
    for name in _INS:
        arr = np.ascontiguousarray(inputs[name])
        arrays[f"in_{name}_dram"] = arr
        args[name] = nc.dram_tensor(f"in_{name}_dram", arr.shape, mybir.dt.from_np(arr.dtype),
                                    kind="ExternalInput").ap()
    out = nc.dram_tensor("out_0_dram", (N_NODES, D), F32, kind="ExternalOutput").ap()
    build(nc, args, out)
    r = run(nc, [arrays], core_ids=[0])
    return r.results[0]["out_0_dram"]
```

```python
from contextlib import ExitStack
import math

import concourse.bass as bass
from concourse import mybir

F32 = mybir.dt.float32
I32 = mybir.dt.int32
ALU = mybir.AluOpType
ACT = mybir.ActivationFunctionType
AX = mybir.AxisListType.X

P = 128
N_NODES = 3125
N_EDGES = 53125
D = 128
DEPTH = 5
RADIAL = 32
CUTOFF = 5.0
EPS = 1e-5
LN2 = math.log(2.0)

CH = 8
GROUP = CH * P
Q = 4
GROUPS = -(-N_EDGES // GROUP)
TURNS = GROUPS // Q
assert GROUPS == TURNS * Q
LAST = N_EDGES - (GROUPS - 1) * GROUP
LAST_P, LAST_J = LAST // CH, LAST % CH
WIN = 80
TILES = -(-N_NODES // P)
BT = 5
BATCHES = TILES // BT
assert TILES == BATCHES * BT
BN = BT * P
NPAD = TILES * P
TAIL = N_NODES - (TILES - 1) * P
MAX_PASSES = -(-N_NODES // WIN)
NEWTON = 3
ROW2 = D + 4


def build(nc, a, out):
    ctx = ExitStack()
    with ctx:
        def sb(name, shape, dt=F32):
            return ctx.enter_context(nc.sbuf_tensor(name, shape, dt))

        def pb(name):
            return ctx.enter_context(nc.psum_tensor(name, [P, 2 * 512], F32))

        def sem(name):
            return ctx.enter_context(nc.semaphore(name))

        table = nc.dram_tensor("table", [NPAD, D], F32, kind="Internal").ap()
        table2 = nc.dram_tensor("table2", [NPAD, ROW2], F32, kind="Internal").ap()

        ident = sb("ident", [P, P])
        ones = sb("ones", [P, P])
        neg_ln2 = sb("neg_ln2", [P, P])
        win_i = sb("win_i", [P, WIN], I32)
        win = sb("win", [P, WIN])
        pass_i = sb("pass_i", [P, MAX_PASSES], I32)
        pass_at = sb("pass_at", [P, MAX_PASSES])
        offset_i = sb("offset_i", [P, 1], I32)
        neg_offset = sb("neg_offset", [P, 1])

        src_i = sb("src_i", [P, (GROUPS + Q) * CH], I32)
        dst_i = sb("dst_i", [P, GROUPS * CH], I32)
        w_e = sb("w_e", [P, GROUPS * CH])
        c_e = sb("c_e", [P, GROUPS * CH])
        c_t = sb("c_t", [P, GROUPS * CH])
        turns_i = sb("turns_i", [P, GROUPS * CH], I32)
        dst0 = sb("dst0", [P, GROUPS * CH])
        dst_rel = sb("dst_rel", [P, GROUPS * CH])
        least = sb("least", [GROUPS, 1])
        most = sb("most", [GROUPS, 1])
        least_b = sb("least_b", [GROUPS, P])
        span_b = sb("span_b", [GROUPS, P])
        base0 = sb("base0", [P, GROUPS])
        base_f = sb("base_f", [P, GROUPS])
        base_i = sb("base_i", [P, GROUPS], I32)
        span_max = sb("span_max", [P, 1])
        pass_hit = sb("pass_hit", [P, MAX_PASSES])
        passes_f = sb("passes_f", [P, 1])
        passes_i = sb("passes_i", [P, 1], I32)
        basis = sb("basis", [P, TURNS * GROUP])
        staged_src = sb("staged_src", [P, Q, CH], I32)
        rows = sb("rows", [P, Q, CH, ROW2])
        table_rows = rows[:, :, :, :].rearrange("p q j w -> p (q j) w")
        onehot = sb("onehot", [P, CH, WIN])
        scatter = sb("scatter", [P, CH, WIN])
        gate = sb("gate", [P, CH, WIN])
        work = sb("work", [P, 4, 2, 512])
        slog = work[:, 0, :, :]
        hidden = work[:, 1, :, :]
        filt = work[:, 2, :, :]
        msg = work[:, 3, :, :]
        node_work = work[:, :, :, :].rearrange("p a h e -> p (a h e)")

        x = sb("x", [P, TILES, D])
        y = sb("y", [P, TILES, D])
        agg = sb("agg", [P, NPAD + WIN])
        deg = sb("deg", [P, NPAD + WIN])
        dst_row = agg[0:GROUPS, 0:GROUP].bitcast(I32)
        score = basis[:, 0:NPAD + WIN]
        deg_col = sb("deg_col", [P, TILES])
        dcol = sb("dcol", [P, TILES])
        stats = sb("stats", [P, TILES, 6])
        mv = sb("mv", [P, TILES, 2])
        var = sb("var", [P, TILES])
        rstd = sb("rstd", [P, TILES])
        newton = sb("newton", [P, TILES])

        w0 = sb("w0", [P, D])
        w3 = sb("w3", [P, D])
        w0T = sb("w0T", [P, D])
        w3T = sb("w3T", [P, D])
        b0 = sb("b0", [P, D])
        b3 = sb("b3", [P, D])
        fw1 = sb("fw1", [P, DEPTH, D])
        fw1_q = sb("fw1_q", [P, Q, D])
        fb1 = sb("fb1", [P, DEPTH])
        fb1_l = sb("fb1_l", [P, 1])
        nfb1 = sb("nfb1", [P, DEPTH])
        nfb1_l = sb("nfb1_l", [P, 1])
        fb1_ln2 = sb("fb1_ln2", [P, DEPTH, P])
        fw2 = sb("fw2", [P, DEPTH, D])
        fb2 = sb("fb2", [P, DEPTH, D])
        lin1 = sb("lin1", [P, DEPTH, D])
        lin2 = sb("lin2", [P, DEPTH, D])
        lb2 = sb("lb2", [P, DEPTH, D])
        ln_g = sb("ln_g", [P, DEPTH, D])
        ln_b = sb("ln_b", [P, DEPTH, D])
        gate_w = sb("gate_w", [P, 2])
        gate_wb = sb("gate_wb", [P, P])
        gate_b = sb("gate_b", [P, 1])

        pA, pB, pC, pD = pb("pA"), pb("pB"), pb("pC"), pb("pD")
        turned_ps = (pA, pB)
        rows_ps = (pC, pD)

        edges_loaded = sem("edges_loaded")
        x_loaded = sem("x_loaded")
        loaded = sem("loaded")
        pads_set = sem("pads_set")
        pool_own = sem("pool_own")
        consts_made = sem("consts_made")
        dve_own = sem("dve_own")
        act_own = sem("act_own")
        spans_spread = sem("spans_spread")
        windows_ps = sem("windows_ps")
        w_turned = sem("w_turned")
        w_taken = sem("w_taken")
        sums_ps = sem("sums_ps")
        basis_w = sem("basis_w")
        offsets_made = sem("offsets_made")
        angle_full = sem("angle_full")
        sine_full = sem("sine_full")
        gathers = [sem(f"gathers{q}") for q in range(Q)]
        gathered = [sem(f"gathered{q}") for q in range(Q)]
        staged = [sem(f"staged{q}") for q in range(Q)]
        first_dma = sem("first_dma")
        table_dma = sem("table_dma")
        table_ready = sem("table_ready")
        scatter_full = sem("scatter_full")
        sum_full = sem("sum_full")
        sum_free = sem("sum_free")
        gate_in = sem("gate_in")
        gate_full = sem("gate_full")
        filter_ready = sem("filter_ready")
        bias_ready = sem("bias_ready")
        deg_full = sem("deg_full")
        deg_ps = sem("deg_ps")
        hid_full = [sem(f"hid_full{h}") for h in range(2)]
        slog_full = [sem(f"slog_full{h}") for h in range(2)]
        ssp_full = [sem(f"ssp_full{h}") for h in range(2)]
        filt_full = [sem(f"filt_full{h}") for h in range(2)]
        msg_full = [sem(f"msg_full{h}") for h in range(2)]
        mean_full = sem("mean_full")
        log_full = sem("log_full")
        v_full = sem("v_full")
        lin_full = sem("lin_full")
        lin_free = sem("lin_free")
        y_full = sem("y_full")
        yT_ps = sem("yT_ps")
        yT_full = sem("yT_full")
        rows_full = sem("rows_full")
        rows_free = sem("rows_free")
        col_full = sem("col_full")
        tab_full = sem("tab_full")
        x_done = sem("x_done")
        stored = sem("stored")

        def per_chunk(tile, at):
            return tile[:, bass.ds(at, CH)].unsqueeze(2).broadcast_to([P, CH, WIN])

        def over_chunks(row):
            return row.unsqueeze(1).broadcast_to([P, CH, WIN])

        def over_tiles(row, n=BT):
            return row.unsqueeze(1).broadcast_to([P, n, D])

        def per_tile(col):
            return col.unsqueeze(2).broadcast_to([P, BT, D])

        def tiles(tile, b):
            return tile[:, b * BT:(b + 1) * BT, :]

        def as_tiles(ps):
            return ps[:, 0:BN].rearrange("p (k d) -> p k d", d=D)

        def nodes(b):
            return slice(b * BN, (b + 1) * BN)

        def tile_nodes(b, k):
            return slice((b * BT + k) * P, (b * BT + k + 1) * P)

        def table_part(tab, b):
            return tab[b * BN:(b + 1) * BN, :].rearrange("(t p) d -> p t d", p=P)

        with nc.Block() as block:

            @block.sync
            def _(sp):
                def load(dst, src, done=edges_loaded):
                    sp.dma_start(dst, src).then_inc(done, 16)

                full = (GROUPS - 1) * GROUP
                sp.wait_ge(pads_set, 1)

                def edges(dst, src):
                    load(dst[:, 0:(GROUPS - 1) * CH].rearrange("p (g j) -> p g j", j=CH),
                         src[0:full].rearrange("(g p j) -> p g j", p=P, j=CH))
                    load(dst[0:LAST_P, (GROUPS - 1) * CH:GROUPS * CH],
                         src[full:full + LAST_P * CH].rearrange("(p j) -> p j", j=CH))
                    load(dst[LAST_P:LAST_P + 1, (GROUPS - 1) * CH:(GROUPS - 1) * CH + LAST_J],
                         src[full + LAST_P * CH:N_EDGES].rearrange("(a j) -> a j", a=1))

                load(x[:, 0:TILES - 1, :], a["x"][0:(TILES - 1) * P, :].rearrange("(t p) d -> p t d", p=P), x_loaded)
                load(x[0:TAIL, TILES - 1, :], a["x"][(TILES - 1) * P:N_NODES, :], x_loaded)
                load(dst_row[0:GROUPS - 1, :], a["dst"][0:full].rearrange("(g e) -> g e", e=GROUP))
                load(dst_row[GROUPS - 1:GROUPS, 0:LAST], a["dst"][full:N_EDGES].rearrange("(a e) -> a e", a=1))
                load(dst_row[GROUPS - 1:GROUPS, LAST:GROUP],
                     a["dst"][N_EDGES - (GROUP - LAST):N_EDGES].rearrange("(a e) -> a e", a=1))
                edges(dst_i, a["dst"])
                edges(src_i, a["src"])
                edges(w_e, a["edge_weight"])
                load(src_i[:, GROUPS * CH:(GROUPS + Q) * CH].rearrange("p (g j) -> p g j", j=CH),
                     a["src"][0:Q * GROUP].rearrange("(g p j) -> p g j", p=P, j=CH))

            N_EDGE_LOADS = 3 + 9 + 1

            @block.gpsimd
            def _(pool):
                pool.memset(ident[:, :], 0.0).then_inc(pool_own, 1)
                pool.iota(win_i[:, :], pattern=[[1, WIN]], base=0, channel_multiplier=0)
                pool.iota(pass_i[:, :], pattern=[[WIN, MAX_PASSES]], base=0, channel_multiplier=0)
                pool.iota(offset_i[:, :], pattern=[[0, 1]], base=0, channel_multiplier=1)
                pool.wait_ge(pool_own, 1)
                pool.sem_inc(pool_own, -1)
                pool.affine_select(out=ident[:, :], in_=ident[:, :], compare_op=ALU.not_equal, fill=1.0,
                                   base=0, pattern=[[-1, P]], channel_multiplier=1).then_inc(consts_made, 1)

            @block.tensor
            def _(pe):
                pe.wait_ge(spans_spread, 1)
                pe.wait_ge(consts_made, 1)
                pe.matmul(pA[:, 0:GROUPS], least_b[:, :], ident[0:GROUPS, 0:GROUPS], start=True, stop=True)
                pe.matmul(pB[:, 0:GROUPS], span_b[:, :], ident[0:GROUPS, 0:GROUPS], start=True, stop=True)\
                  .then_inc(windows_ps, 1)

            @block.vector
            def _(dve):
                def own(ins):
                    ins.then_inc(dve_own, 1)
                    dve.wait_ge(dve_own, 1)
                    dve.sem_inc(dve_own, -1)

                dve.memset(src_i[:, :], 0)
                dve.memset(dst_i[:, :], -1)
                dve.memset(w_e[:, :], 0.0)
                dve.memset(x[:, TILES - 1, :], 0.0).then_inc(pads_set, 1)
                dve.memset(ones[:, :], 1.0)
                dve.memset(neg_ln2[:, :], -LN2)
                dve.memset(fw1_q[:, :, :], 0.0)
                dve.memset(basis[(Q - 1) * RADIAL:P, (TURNS - 1) * GROUP + LAST:TURNS * GROUP], 0.0)
                dve.memset(deg[:, :], 0.0)
                dve.memset(rows[:, :, :, D:ROW2], 0.0)
                dve.wait_ge(consts_made, 1)
                dve.tensor_copy(win[:, :], win_i[:, :])
                dve.tensor_copy(pass_at[:, :], pass_i[:, :])
                own(dve.tensor_scalar(offset_i[:, :], offset_i[:, :], RADIAL - 1, None, ALU.bitwise_and))
                dve.tensor_scalar(neg_offset[:, :], offset_i[:, :], -CUTOFF / (RADIAL - 1), None, ALU.mult)
                dve.wait_ge(edges_loaded, 16 * N_EDGE_LOADS)
                for q in range(Q):
                    dve.tensor_copy(staged_src[:, q, :], src_i[:, q * CH:(q + 1) * CH])
                dve.tensor_reduce(least[:, :], dst_row[:, :], AX, ALU.min)
                own(dve.tensor_reduce(most[:, :], dst_row[:, :], AX, ALU.max))
                own(dve.tensor_tensor(most[:, :], most[:, :], least[:, :], ALU.subtract))
                dve.tensor_copy(least_b[:, :], least[:, 0:1].broadcast_to([GROUPS, P]))
                dve.tensor_copy(span_b[:, :], most[:, 0:1].broadcast_to([GROUPS, P])).then_inc(spans_spread, 1)
                dve.tensor_copy(dst0[:, :], dst_i[:, :])
                dve.wait_ge(windows_ps, 1)
                dve.tensor_copy(base0[:, :], pA[:, 0:GROUPS])
                own(dve.tensor_reduce(span_max[:, :], pB[:, 0:GROUPS], AX, ALU.max))
                own(dve.tensor_scalar(pass_hit[:, :], pass_at[:, :], span_max[:, 0:1], None, ALU.is_le))
                own(dve.tensor_reduce(passes_f[:, :], pass_hit[:, :], AX, ALU.add))
                dve.tensor_copy(passes_i[:, :], passes_f[:, :])
                dst0_g = dst0[:, :].rearrange("p (g j) -> p g j", j=CH)
                dve.tensor_tensor(dst0_g, dst0_g, base0[:, :].unsqueeze(2).broadcast_to([P, GROUPS, CH]), ALU.subtract)

        with nc.Block() as block:

            @block.sync
            def _(sp):
                def load(dst, src, turned=False):
                    sp.dma_start(dst, src, allow_slow_non_contiguous=turned).then_inc(loaded, 16)

                load(w0[:, :], a["L0_gnn_W"])
                load(w3[:, :], a["L3_gnn_W"])
                load(b0[:, :], a["L0_gnn_b"].partition_broadcast(P))
                load(b3[:, :], a["L3_gnn_b"].partition_broadcast(P))
                for q in range(Q):
                    load(fw1[q * RADIAL:(q + 1) * RADIAL, :, :], a["L1_gnn_fw1"].rearrange("l r d -> r l d"))
                load(fb1[:, :], a["L1_gnn_fb1"].rearrange("l d -> d l"), turned=True)
                load(fw2[:, :, :], a["L1_gnn_fw2"].rearrange("l k d -> k l d"))
                load(lin1[:, :, :], a["L1_gnn_lin1_w"].rearrange("l k d -> k l d"))
                load(lin2[:, :, :], a["L1_gnn_lin2_w"].rearrange("l k d -> k l d"))
                for dst, src in ((fb2, "fb2"), (lb2, "lin2_b"), (ln_g, "ln_g"), (ln_b, "ln_b")):
                    load(dst[:, :, :], a["L1_gnn_" + src].partition_broadcast(P))
                load(gate_w[:, :], a["L2_gnn_gate_w"].rearrange("a (s d) -> d (a s)", d=D), turned=True)
                load(gate_b[:, :], a["L2_gnn_gate_b"].partition_broadcast(P))
                n_pass = sp.value_load(passes_i[0:1, 0:1], min_val=1, max_val=MAX_PASSES)
                with sp.Fori(0, n_pass * ((DEPTH + 3) * TURNS)) as n:
                    for q in range(Q):
                        sp.wait_ge(gathers[q], n * (CH * 16) + CH * 16)
                        sp.sem_inc(gathered[q], 1)
                for b in range(BATCHES):
                    sp.wait_ge(x_done, 1)
                    sp.sem_inc(x_done, -1)
                    n = BT if b < BATCHES - 1 else BT - 1
                    sp.dma_start(out[b * BN:b * BN + n * P, :].rearrange("(t p) d -> p t d", p=P),
                                 x[:, b * BT:b * BT + n, :]).then_inc(stored, 16)
                sp.dma_start(out[(TILES - 1) * P:N_NODES, :], x[0:TAIL, TILES - 1, :]).then_inc(stored, 16)
                sp.wait_ge(stored, 16 * (BATCHES + 1))

            N_LOADS = 4 + Q + 4 + 4 + 2

            @block.gpsimd
            def _(pool):
                n_pass = pool.value_load(passes_i[0:1, 0:1], min_val=1, max_val=MAX_PASSES)

                def gather(tab, width):
                    pool.wait_ge(table_ready, 1)
                    pool.sem_inc(table_ready, -1)
                    with pool.Fori(0, n_pass):
                        with pool.Fori(0, TURNS):
                            for q in range(Q):
                                pool.wait_ge(staged[q], 1)
                                pool.sem_inc(staged[q], -1)
                                for j in range(CH):
                                    pool.indirect_dma_start(
                                        out=rows[:, q, j, 0:width], out_offset=None, in_=tab[:, :],
                                        in_offset=bass.IndirectOffsetOnAxis(ap=staged_src[:, q, j:j + 1], axis=0),
                                    ).then_inc(gathers[q], 16)

                gather(table, D)
                with pool.Fori(0, DEPTH):
                    gather(table, D)
                gather(table2, ROW2)
                gather(table, D)

            @block.tensor
            def _(pe):
                n_pass = pe.value_load(passes_i[0:1, 0:1], min_val=1, max_val=MAX_PASSES)

                def prepare_weights():
                    pe.wait_ge(loaded, 16 * N_LOADS)
                    pe.transpose(pA[:, 0:P], w0[:, :], ident[:, :])
                    pe.transpose(pB[:, 0:P], w3[:, :], ident[:, :]).then_inc(w_turned, 1)
                    pe.wait_ge(w_taken, 1)
                    pe.sem_inc(w_taken, -1)
                    for l in range(DEPTH):
                        pe.matmul(pA[:, l * D:(l + 1) * D], fb1_ln2[:, l, :], fw2[:, l, :], start=True, stop=True)
                        last = pe.matmul(pB[:, l * D:(l + 1) * D], neg_ln2[:, :], lin2[:, l, :], start=True, stop=True)
                    last.then_inc(sums_ps, 1)

                def plain_edges(degrees=False):
                    with pe.Fori(0, n_pass):
                        with pe.Fori(0, TURNS):
                            for q in range(Q):
                                pe.wait_ge(scatter_full, 1)
                                pe.sem_inc(scatter_full, -1)
                                pe.wait_ge(sum_free, 1)
                                pe.sem_inc(sum_free, -1)
                                if degrees:
                                    for j in range(CH):
                                        pe.matmul(pD[:, 0:WIN], ones[:, :], onehot[:, j, :],
                                                  start=(j == 0), stop=(j == CH - 1))
                                for j in range(CH):
                                    mm = pe.matmul(pC[:, 0:WIN], rows[:, q, j, 0:D], scatter[:, j, :],
                                                   start=(j == 0), stop=(j == CH - 1))
                                mm.then_inc(sum_full, 1)

                def hidden_units(i, q, h):
                    pe.matmul(pA[:, h * 512:(h + 1) * 512], fw1_q[:, q, :],
                              basis[:, bass.ds(i * GROUP + h, 512, 2)], start=True, stop=True).then_inc(hid_full[h], 1)

                def conv_turn(l, i, last):
                    for q in range(Q):
                        for h in range(2):
                            pe.wait_ge(ssp_full[h], 1)
                            pe.sem_inc(ssp_full[h], -1)
                            for c in range(CH // 2):
                                mm = pe.matmul(pB[:, h * 512 + c * D:h * 512 + (c + 1) * D],
                                               hidden[:, h, c:512:CH // 2], fw2[:, l, :], start=True, stop=True)
                            mm.then_inc(filt_full[h], 1)
                            if q < Q - 1:
                                hidden_units(i, q + 1, h)
                            elif not last:
                                hidden_units(i + 1, 0, h)
                        pe.wait_ge(scatter_full, 1)
                        pe.sem_inc(scatter_full, -1)
                        pe.wait_ge(sum_free, 1)
                        pe.sem_inc(sum_free, -1)
                        for h in range(2):
                            pe.wait_ge(msg_full[h], 1)
                            pe.sem_inc(msg_full[h], -1)
                            for c in range(CH // 2):
                                mm = pe.matmul(pC[:, 0:WIN], msg[:, h, c * D:(c + 1) * D], scatter[:, 2 * c + h, :],
                                               start=(h == 0 and c == 0), stop=(h == 1 and c == CH // 2 - 1))
                        mm.then_inc(sum_full, 1)

                def conv_edges(l):
                    pe.wait_ge(filter_ready, 1)
                    pe.sem_inc(filter_ready, -1)
                    with pe.Fori(0, n_pass):
                        for h in range(2):
                            hidden_units(0, 0, h)
                        with pe.Fori(0, TURNS - 1) as i:
                            conv_turn(l, i, last=False)
                        conv_turn(l, TURNS - 1, last=True)

                def linear(weights, ready=None):
                    for b in range(BATCHES):
                        if ready is not None:
                            pe.wait_ge(ready, 1)
                            pe.sem_inc(ready, -1)
                        if b >= 2:
                            pe.wait_ge(lin_free, 1)
                            pe.sem_inc(lin_free, -1)
                        ps = turned_ps[b % 2]
                        for k in range(BT):
                            to, at = ps[:, k * D:(k + 1) * D], agg[:, tile_nodes(b, k)]
                            mm = pe.transpose(to, at, ident[:, :]) if weights is None else \
                                pe.matmul(to, at, weights, start=True, stop=True)
                        mm.then_inc(lin_full, 1)

                def through_turned(lin_before, use):
                    for b in range(BATCHES + 1):
                        if b < BATCHES:
                            pe.wait_ge(y_full, 1)
                            pe.sem_inc(y_full, -1)
                            if b < 2 and lin_before:
                                pe.wait_ge(lin_free, 1)
                                pe.sem_inc(lin_free, -1)
                            for k in range(BT):
                                mm = pe.transpose(turned_ps[b % 2][:, k * P:(k + 1) * P], y[:, b * BT + k, :], ident[:, :])
                            mm.then_inc(yT_ps, 1)
                        if b >= 1:
                            pe.wait_ge(yT_full, 1)
                            pe.sem_inc(yT_full, -1)
                            use(b - 1)

                def next_table(weights):
                    def use(b):
                        if b >= 2:
                            pe.wait_ge(rows_free, 1)
                            pe.sem_inc(rows_free, -1)
                        for k in range(BT):
                            mm = pe.matmul(rows_ps[b % 2][:, k * D:(k + 1) * D], node_work[:, tile_nodes(b, k)], weights,
                                           start=True, stop=True)
                        mm.then_inc(rows_full, 1)
                    through_turned(True, use)
                    pe.wait_ge(rows_free, 2)
                    pe.sem_inc(rows_free, -2)

                prepare_weights()
                plain_edges(degrees=True)
                pe.wait_ge(deg_full, 1)
                pe.sem_inc(deg_full, -1)
                for t in range(TILES):
                    mm = pe.matmul(pD[:, t:t + 1], deg[0:1, t * P:(t + 1) * P], ones[0:1, 0:1], start=True, stop=True)
                mm.then_inc(deg_ps, 1)
                linear(w0T[:, :])
                next_table(lin1[:, 0, :])
                with pe.Fori(0, DEPTH - 1) as l:
                    conv_edges(l)
                    linear(lin2[:, l, :], v_full)
                    next_table(lin1[:, l + 1, :])
                conv_edges(DEPTH - 1)
                linear(lin2[:, DEPTH - 1, :], v_full)

                def scores(b):
                    if b >= 2:
                        pe.wait_ge(rows_free, 1)
                        pe.sem_inc(rows_free, -1)
                    yT = node_work[:, nodes(b)]
                    ps = rows_ps[b % 2]
                    pe.matmul(ps[:, 0:512], gate_wb[:, :], yT[:, 0:512], start=True, stop=True)
                    pe.matmul(ps[:, 512:BN], gate_wb[:, :], yT[:, 512:BN], start=True, stop=True)
                    for k in range(BT):
                        mm = pe.matmul(ps[:, BN + k:BN + k + 1], yT[:, k * P:(k + 1) * P], gate_w[:, 1:2],
                                       start=True, stop=True)
                    mm.then_inc(col_full, 1)

                through_turned(True, scores)
                pe.wait_ge(rows_free, 2)
                pe.sem_inc(rows_free, -2)
                plain_edges()
                linear(None)
                pe.wait_ge(lin_free, 2)
                pe.sem_inc(lin_free, -2)
                plain_edges()
                linear(w3T[:, :])
                pe.wait_ge(lin_free, 2)
                pe.sem_inc(lin_free, -2)

            @block.scalar
            def _(act):
                n_pass = act.value_load(passes_i[0:1, 0:1], min_val=1, max_val=MAX_PASSES)

                def own(ins):
                    ins.then_inc(act_own, 1)
                    act.wait_ge(act_own, 1)
                    act.sem_inc(act_own, -1)

                def basis_of_edges():
                    for q in range(Q):
                        n = TURNS if q < Q - 1 else TURNS - 1
                        act.dma_start(
                            basis[q * RADIAL:(q + 1) * RADIAL, 0:n * GROUP].rearrange("r (i e) -> r i e", e=GROUP),
                            a["edge_weight"][0:(GROUPS - 1) * GROUP]
                            .rearrange("(i s e) -> i s e", s=1, e=GROUP)[q:(n - 1) * Q + q + 1:Q, 0, :]
                            .partition_broadcast(RADIAL)).then_inc(basis_w, 16)
                    act.dma_start(basis[(Q - 1) * RADIAL:P, (TURNS - 1) * GROUP:(TURNS - 1) * GROUP + LAST],
                                  a["edge_weight"][(GROUPS - 1) * GROUP:N_EDGES].partition_broadcast(RADIAL))\
                       .then_inc(basis_w, 16)
                    act.wait_ge(angle_full, 1)
                    act.sem_inc(angle_full, -1)
                    act.activation(c_t[:, :], c_e[:, :], ACT.Sin, scale=math.pi / (2 * CUTOFF)).then_inc(sine_full, 1)
                    act.preload_act_table_set("natural_log_exp_and_others")
                    act.wait_ge(basis_w, 16 * (Q + 1))
                    own(act.activation(basis[:, :], basis[:, :], ACT.Square, bias=neg_offset[:, 0:1]))
                    step = CUTOFF / (RADIAL - 1)
                    own(act.activation(basis[:, :], basis[:, :], ACT.Exp, scale=-0.5 / (step * step)))

                def softplus_log(dst, arg, full, **bias):
                    own(act.activation(dst, arg, ACT.Abs, **bias))
                    own(act.activation(dst, dst, ACT.Exp, scale=-1.0))
                    act.activation(dst, dst, ACT.Ln, bias=1.0).then_inc(full, 1)

                def write_table(tab, width, b):
                    act.dma_start(table_part(tab, b), tiles(table_rows, b)[:, :, 0:width]).then_inc(table_dma, 16)

                def table_written():
                    act.wait_ge(table_dma, 16 * BATCHES)
                    act.sem_inc(table_dma, -16 * BATCHES)
                    act.sem_inc(table_ready, 1)

                def written_by_vector(tab, width):
                    for b in range(BATCHES):
                        act.wait_ge(tab_full, 1)
                        act.sem_inc(tab_full, -1)
                        write_table(tab, width, b)
                    table_written()

                def turned(b):
                    act.wait_ge(yT_ps, 1)
                    act.sem_inc(yT_ps, -1)
                    act.activation(node_work[:, nodes(b)], turned_ps[b % 2][:, 0:BN], ACT.Copy).then_inc(yT_full, 1)

                def next_table():
                    for b in range(BATCHES + 1):
                        if b < BATCHES:
                            turned(b)
                        if b >= 1:
                            act.wait_ge(rows_full, 1)
                            act.sem_inc(rows_full, -1)
                            own(act.activation(tiles(table_rows, b - 1)[:, :, 0:D], as_tiles(rows_ps[(b - 1) % 2]), ACT.Copy))
                            act.sem_inc(rows_free, 1)
                            write_table(table, D, b - 1)
                    table_written()

                def conv_edges():
                    act.wait_ge(bias_ready, 1)
                    act.sem_inc(bias_ready, -1)
                    with act.Fori(0, n_pass):
                        with act.Fori(0, TURNS):
                            for q in range(Q):
                                for h in range(2):
                                    act.wait_ge(hid_full[h], 1)
                                    act.sem_inc(hid_full[h], -1)
                                    softplus_log(slog[:, h, :], pA[:, h * 512:(h + 1) * 512], slog_full[h],
                                                 bias=fb1_l[:, 0:1])
                    for b in range(BATCHES):
                        act.wait_ge(mean_full, 1)
                        act.sem_inc(mean_full, -1)
                        softplus_log(node_work[:, nodes(b)], agg[:, nodes(b)], log_full)

                written_by_vector(table, D)
                basis_of_edges()
                next_table()
                act.preload_act_table_set("natural_log_exp_and_others")
                with act.Fori(0, DEPTH - 1):
                    conv_edges()
                    next_table()
                conv_edges()
                for b in range(BATCHES + 1):
                    if b < BATCHES:
                        turned(b)
                    if b >= 1:
                        act.wait_ge(tab_full, 1)
                        act.sem_inc(tab_full, -1)
                        own(act.activation(score[:, nodes(b - 1)], rows_ps[(b - 1) % 2][:, 0:BN], ACT.Copy))
                        act.sem_inc(rows_free, 1)
                        write_table(table2, ROW2, b - 1)
                table_written()
                with act.Fori(0, n_pass):
                    with act.Fori(0, TURNS):
                        for q in range(Q):
                            act.wait_ge(gate_in, 1)
                            act.sem_inc(gate_in, -1)
                            act.activation(gate[:, :, :], gate[:, :, :], ACT.Tanh).then_inc(gate_full, 1)
                written_by_vector(table, D)

            @block.vector
            def _(dve):
                n_pass = dve.value_load(passes_i[0:1, 0:1], min_val=1, max_val=MAX_PASSES)

                def own(ins):
                    ins.then_inc(dve_own, 1)
                    dve.wait_ge(dve_own, 1)
                    dve.sem_inc(dve_own, -1)

                for q in range(Q):
                    dve.sem_inc(staged[q], 1)
                dve.sem_inc(sum_free, 1)

                def prepare_weights():
                    own(dve.tensor_scalar(turns_i[:, :], w_e[:, :], 1.0 / (2 * CUTOFF), None, ALU.mult))
                    own(dve.scalar_tensor_tensor(c_e[:, :], turns_i[:, :], -2 * CUTOFF, w_e[:, :], ALU.mult, ALU.add))
                    dve.sem_inc(angle_full, 1)
                    dve.wait_ge(loaded, 16 * N_LOADS)
                    dve.tensor_scalar(nfb1[:, :], fb1[:, :], -1.0, None, ALU.mult)
                    dve.tensor_scalar(fb1_ln2[:, :, :], fb1[:, :].unsqueeze(2).broadcast_to([P, DEPTH, P]), -LN2, None,
                                      ALU.add)
                    dve.tensor_copy(gate_wb[:, :], gate_w[:, 0:1].broadcast_to([P, P]))
                    dve.wait_ge(w_turned, 1)
                    dve.sem_inc(w_turned, -1)
                    dve.tensor_copy(w0T[:, :], pA[:, 0:P])
                    dve.tensor_copy(w3T[:, :], pB[:, 0:P]).then_inc(w_taken, 1)
                    dve.wait_ge(sine_full, 1)
                    dve.sem_inc(sine_full, -1)
                    own(dve.tensor_tensor(c_t[:, :], c_t[:, :], c_t[:, :], ALU.mult))
                    own(dve.tensor_scalar(c_t[:, :], c_t[:, :], -1.0, 1.0, ALU.mult, ALU.add))
                    own(dve.tensor_scalar(c_e[:, :], w_e[:, :], CUTOFF, None, ALU.is_lt))
                    dve.tensor_tensor(c_e[:, :], c_e[:, :], c_t[:, :], ALU.mult)
                    dve.wait_ge(sums_ps, 1)
                    dve.sem_inc(sums_ps, -1)
                    for bias, ps in ((fb2, pA), (lb2, pB)):
                        flat = bias[:, :, :].rearrange("p l d -> p (l d)")
                        ins = dve.tensor_tensor(flat, flat, ps[:, 0:DEPTH * D], ALU.add)
                    own(ins)

                def start_sums():
                    dve.memset(agg[:, :], 0.0)
                    dve.tensor_copy(dst_rel[:, :], dst0[:, :])
                    dve.tensor_copy(base_f[:, :], base0[:, :])
                    own(dve.tensor_copy(base_i[:, :], base0[:, :]))

                def next_pass():
                    dve.tensor_scalar(dst_rel[:, :], dst_rel[:, :], -float(WIN), None, ALU.add)
                    own(dve.tensor_scalar(base_f[:, :], base_f[:, :], float(WIN), float(NPAD), ALU.add, ALU.min))
                    own(dve.tensor_copy(base_i[:, :], base_f[:, :]))

                def window_start(i, q):
                    return dve.value_load(base_i[0:1, bass.ds(i * Q + q, 1)], min_val=0, max_val=NPAD)

                def match(dst, at):
                    return dve.tensor_tensor(dst[:, :, :], over_chunks(win[:, :]), per_chunk(dst_rel, at), ALU.is_equal)

                def add_sums(i, q, base, degrees=False):
                    dve.wait_ge(sum_full, 1)
                    dve.sem_inc(sum_full, -1)
                    dve.tensor_copy(staged_src[:, q, :], src_i[:, bass.ds(i * (Q * CH) + (Q + q) * CH, CH)])\
                       .then_inc(staged[q], 1)
                    if degrees:
                        own(dve.tensor_tensor(deg[:, bass.ds(base, WIN)], deg[:, bass.ds(base, WIN)], pD[:, 0:WIN], ALU.add))
                    dve.tensor_tensor(agg[:, bass.ds(base, WIN)], agg[:, bass.ds(base, WIN)], pC[:, 0:WIN], ALU.add)\
                       .then_inc(sum_free, 1)

                def last_sum():
                    dve.wait_ge(sum_free, 1)

                def plain_edges(kind):
                    with dve.Fori(0, n_pass):
                        with dve.Fori(0, TURNS) as i:
                            for q in range(Q):
                                at = i * (Q * CH) + q * CH
                                base = window_start(i, q)
                                dve.wait_ge(gathered[q], 1)
                                dve.sem_inc(gathered[q], -1)
                                if kind == "count":
                                    match(scatter, at).then_inc(scatter_full, 1)
                                elif kind == "weight":
                                    own(match(onehot, at))
                                    dve.tensor_tensor(scatter[:, :, :], onehot[:, :, :], per_chunk(w_e, at), ALU.mult)\
                                       .then_inc(scatter_full, 1)
                                else:
                                    dve.tensor_tensor(gate[:, :, :], over_chunks(score[:, bass.ds(base, WIN)]),
                                                      rows[:, q, :, D:D + 1].broadcast_to([P, CH, WIN]), ALU.add)\
                                       .then_inc(gate_in, 1)
                                    own(match(onehot, at))
                                    own(dve.tensor_tensor(onehot[:, :, :], onehot[:, :, :], per_chunk(w_e, at), ALU.mult))
                                    dve.wait_ge(gate_full, 1)
                                    dve.sem_inc(gate_full, -1)
                                    dve.tensor_tensor(scatter[:, :, :], onehot[:, :, :], gate[:, :, :], ALU.mult)\
                                       .then_inc(scatter_full, 1)
                                add_sums(i, q, base, degrees=(kind == "weight"))
                        next_pass()
                    last_sum()

                def softplus_rest(h):
                    dve.wait_ge(slog_full[h], 1)
                    dve.sem_inc(slog_full[h], -1)
                    dve.scalar_tensor_tensor(hidden[:, h, :], pA[:, h * 512:(h + 1) * 512], nfb1_l[:, 0:1],
                                             slog[:, h, :], ALU.max, ALU.add).then_inc(ssp_full[h], 1)

                def conv_turn(l, i, last):
                    for q in range(Q):
                        at = i * (Q * CH) + q * CH
                        base = window_start(i, q)
                        own(match(onehot, at))
                        dve.tensor_tensor(scatter[:, :, :], onehot[:, :, :], per_chunk(c_e, at), ALU.mult)\
                           .then_inc(scatter_full, 1)
                        for h in range(2):
                            dve.wait_ge(filt_full[h], 1)
                            dve.sem_inc(filt_full[h], -1)
                            f4 = filt[:, h, :].rearrange("p (c d) -> p c d", d=D)
                            own(dve.tensor_tensor(
                                f4, pB[:, h * 512:(h + 1) * 512].rearrange("p (c d) -> p c d", d=D),
                                over_tiles(fb2[:, l, :], CH // 2), ALU.add))
                            if h == 0:
                                dve.wait_ge(gathered[q], 1)
                                dve.sem_inc(gathered[q], -1)
                            dve.tensor_tensor(msg[:, h, :].rearrange("p (c d) -> p c d", d=D), f4,
                                              rows[:, q, h:CH:2, 0:D], ALU.mult).then_inc(msg_full[h], 1)
                        if not (last and q == Q - 1):
                            for h in range(2):
                                softplus_rest(h)
                        add_sums(i, q, base)

                def conv_edges(l):
                    for q in range(Q):
                        dve.tensor_copy(fw1_q[q * RADIAL:(q + 1) * RADIAL, q, :], fw1[q * RADIAL:(q + 1) * RADIAL, l, :])
                    dve.tensor_copy(nfb1_l[:, :], nfb1[:, bass.ds(l, 1)]).then_inc(filter_ready, 1)
                    own(dve.tensor_copy(fb1_l[:, :], fb1[:, bass.ds(l, 1)]))
                    dve.sem_inc(bias_ready, 1)
                    start_sums()
                    dve.wait_ge(slog_full[0], 1)
                    dve.tensor_tensor(y[:, :, :], y[:, :, :], over_tiles(lb2[:, l, :], TILES), ALU.add)
                    with dve.Fori(0, n_pass):
                        for h in range(2):
                            softplus_rest(h)
                        with dve.Fori(0, TURNS - 1) as i:
                            conv_turn(l, i, last=False)
                        conv_turn(l, TURNS - 1, last=True)
                        next_pass()
                    last_sum()

                def rsqrt(root, arg):
                    tmp = newton[:, :]
                    own(dve.tensor_scalar(tmp.bitcast(I32), arg.bitcast(I32), 1, None, ALU.logical_shift_right))
                    own(dve.tensor_scalar(root.bitcast(I32), tmp.bitcast(I32), -1.0, float(0x5F3759DF), ALU.mult, ALU.add))
                    for _ in range(NEWTON):
                        own(dve.scalar_tensor_tensor(tmp, root, -0.5, root, ALU.mult, ALU.mult))
                        own(dve.tensor_tensor(tmp, tmp, arg, ALU.mult))
                        own(dve.scalar_tensor_tensor(root, tmp, 1.5, root, ALU.add, ALU.mult))

                def statistics(state, b):
                    for t in range(b * BT, (b + 1) * BT):
                        ins = dve.bn_stats(stats[:, t, :], state[:, t, :])
                    return ins

                def deviations():
                    for t in range(TILES):
                        ins = dve.bn_aggr(mv[:, t, :], stats[:, t, :])
                    own(ins)
                    own(dve.tensor_scalar(var[:, :], mv[:, :, 1], EPS, None, ALU.add))
                    rsqrt(rstd[:, :], var[:, :])

                def normalise(dst, state, b):
                    for k in range(BT):
                        t = b * BT + k
                        ins = dve.tensor_scalar(dst[:, k, :], state[:, t, :], mv[:, t, 0:1], rstd[:, t:t + 1],
                                                ALU.subtract, ALU.mult)
                    own(ins)

                def relu(tile):
                    return dve.tensor_scalar(tile, tile, 0.0, None, ALU.max)

                def relu_norm_to_y():
                    deviations()
                    for b in range(BATCHES):
                        normalise(tiles(y, b), x, b)
                        relu(tiles(y, b)).then_inc(y_full, 1)

                def relu_norm_to_table():
                    deviations()
                    for b in range(BATCHES):
                        part = tiles(table_rows, b)[:, :, 0:D]
                        normalise(part, x, b)
                        relu(part).then_inc(tab_full, 1)

                dve.wait_ge(x_loaded, 32)
                for b in range(BATCHES):
                    ins = statistics(x, b)
                own(ins)
                relu_norm_to_table()
                start_sums()
                prepare_weights()
                dve.tensor_tensor(x[:, :, :], x[:, :, :], over_tiles(b0[:, :], TILES), ALU.add)
                plain_edges("weight")
                dve.sem_inc(deg_full, 1)
                dve.wait_ge(deg_ps, 1)
                dve.sem_inc(deg_ps, -1)
                own(dve.tensor_scalar(deg_col[:, :], pD[:, 0:TILES], 1.0, None, ALU.max))
                for b in range(BATCHES):
                    dve.wait_ge(lin_full, 1)
                    dve.sem_inc(lin_full, -1)
                    own(dve.tensor_tensor(tiles(x, b), as_tiles(turned_ps[b % 2]), tiles(x, b), ALU.add))
                    dve.sem_inc(lin_free, 1)
                    ins = statistics(x, b)
                own(ins)
                relu_norm_to_y()
                rsqrt(dcol[:, :], deg_col[:, :])
                own(dve.tensor_scalar(deg[:, :], deg[:, :], 1.0, None, ALU.max))
                own(dve.reciprocal(deg[:, :], deg[:, :]))

                def conv_layer(l, last):
                    conv_edges(l)
                    for b in range(BATCHES):
                        own(dve.tensor_tensor(agg[:, nodes(b)], agg[:, nodes(b)], deg[:, nodes(b)], ALU.mult))
                        dve.sem_inc(mean_full, 1)
                    for b in range(BATCHES + 1):
                        if b < BATCHES:
                            dve.wait_ge(log_full, 1)
                            dve.sem_inc(log_full, -1)
                            dve.scalar_tensor_tensor(agg[:, nodes(b)], agg[:, nodes(b)], 0.0, node_work[:, nodes(b)],
                                                     ALU.max, ALU.add).then_inc(v_full, 1)
                        if b >= 1:
                            dve.wait_ge(lin_full, 1)
                            dve.sem_inc(lin_full, -1)
                            own(dve.tensor_tensor(tiles(y, b - 1), as_tiles(turned_ps[(b - 1) % 2]), tiles(y, b - 1), ALU.add))
                            dve.sem_inc(lin_free, 1)
                            ins = statistics(y, b - 1)
                    own(ins)
                    deviations()
                    for b in range(BATCHES):
                        normalise(tiles(y, b), y, b)
                        own(dve.tensor_tensor(tiles(y, b), tiles(y, b), over_tiles(ln_g[:, l, :]), ALU.mult))
                        ins = dve.tensor_tensor(tiles(y, b), tiles(y, b), over_tiles(ln_b[:, l, :]), ALU.add)
                        if not last:
                            ins.then_inc(y_full, 1)
                    if last:
                        own(ins)

                with dve.Fori(0, DEPTH - 1) as l:
                    conv_layer(l, last=False)
                conv_layer(DEPTH - 1, last=True)

                own(dve.memset(score[:, NPAD:NPAD + WIN], 0.0))
                own(dve.tensor_tensor(x[:, :, :], x[:, :, :], y[:, :, :], ALU.add))
                for b in range(BATCHES):
                    ins = statistics(x, b)
                own(ins)
                relu_norm_to_y()
                for b in range(BATCHES):
                    part = tiles(table_rows, b)
                    own(dve.tensor_tensor(part[:, :, 0:D], tiles(y, b), per_tile(dcol[:, b * BT:(b + 1) * BT]), ALU.mult))
                    dve.wait_ge(col_full, 1)
                    dve.sem_inc(col_full, -1)
                    dve.tensor_scalar(part[:, :, D:D + 1], rows_ps[b % 2][:, BN:BN + BT].unsqueeze(2), gate_b[:, 0:1], None,
                                      ALU.add).then_inc(tab_full, 1)
                start_sums()
                plain_edges("gate")
                for b in range(BATCHES):
                    dve.wait_ge(lin_full, 1)
                    dve.sem_inc(lin_full, -1)
                    z5 = node_work[:, nodes(b)].rearrange("p (k d) -> p k d", d=D)
                    own(dve.tensor_tensor(z5, as_tiles(turned_ps[b % 2]), per_tile(dcol[:, b * BT:(b + 1) * BT]), ALU.mult))
                    dve.sem_inc(lin_free, 1)
                    own(dve.tensor_tensor(tiles(x, b), z5, tiles(x, b), ALU.add))
                    ins = statistics(x, b)
                own(ins)
                relu_norm_to_table()

                start_sums()
                dve.tensor_tensor(x[:, :, :], x[:, :, :], over_tiles(b3[:, :], TILES), ALU.add)
                plain_edges("count")
                for b in range(BATCHES):
                    dve.wait_ge(lin_full, 1)
                    dve.sem_inc(lin_full, -1)
                    own(dve.tensor_tensor(tiles(x, b), as_tiles(turned_ps[b % 2]), tiles(x, b), ALU.add))
                    dve.sem_inc(lin_free, 1)
                    dve.sem_inc(x_done, 1)


_INS = ['x', 'src', 'dst', 'edge_weight', 'L0_gnn_W', 'L0_gnn_b', 'L1_gnn_fw1', 'L1_gnn_fb1', 'L1_gnn_fw2',
        'L1_gnn_fb2', 'L1_gnn_lin1_w', 'L1_gnn_lin2_w', 'L1_gnn_lin2_b', 'L1_gnn_ln_g', 'L1_gnn_ln_b',
        'L2_gnn_gate_w', 'L2_gnn_gate_b', 'L3_gnn_W', 'L3_gnn_b']


def kernel(**inputs):
    import numpy as np
    import concourse.bacc as bacc
    from concourse.bass_utils import run_bass_kernel_spmd as run

    nc = bacc.Bacc("TRN2", target_bir_lowering=False, num_devices=1)
    arrays, args = {}, {}
    for name in _INS:
        arr = np.ascontiguousarray(inputs[name])
        arrays[f"in_{name}_dram"] = arr
        args[name] = nc.dram_tensor(f"in_{name}_dram", arr.shape, mybir.dt.from_np(arr.dtype),
                                    kind="ExternalInput").ap()
    out = nc.dram_tensor("out_0_dram", (N_NODES, D), F32, kind="ExternalOutput").ap()
    build(nc, args, out)
    r = run(nc, [arrays], core_ids=[0])
    return r.results[0]["out_0_dram"]
```

```python
from contextlib import ExitStack
import math

import concourse.bass as bass
from concourse import mybir

F32 = mybir.dt.float32
I32 = mybir.dt.int32
BF16 = mybir.dt.bfloat16
ALU = mybir.AluOpType
ACT = mybir.ActivationFunctionType
AX = mybir.AxisListType.X

P = 128
N_NODES = 3125
N_EDGES = 53125
D = 128
DEPTH = 5
RADIAL = 32
CUTOFF = 5.0
EPS = 1e-5
LN2 = math.log(2.0)

CH = 8
GROUP = CH * P
Q = 4
GROUPS = -(-N_EDGES // GROUP)
TURNS = GROUPS // Q
assert GROUPS == TURNS * Q
LAST = N_EDGES - (GROUPS - 1) * GROUP
LAST_P, LAST_J = LAST // CH, LAST % CH
WIN = 80
TILES = -(-N_NODES // P)
SIZES = (3, 6, 6, 6, 4)
FIRST = tuple(sum(SIZES[:b]) for b in range(len(SIZES)))
BATCHES = len(SIZES)
assert sum(SIZES) == TILES and max(SIZES) * P <= 2 * 512
NPAD = TILES * P
TAIL = N_NODES - (TILES - 1) * P
MAX_PASSES = -(-N_NODES // WIN)
POOL_MEANS = (2, 3, 4)
POOL_BATCHES = (3, 4)
ROW2 = D + 4


def build(nc, a, out):
    ctx = ExitStack()
    with ctx:
        def sb(name, shape, dt=F32):
            return ctx.enter_context(nc.sbuf_tensor(name, shape, dt))

        def pb(name):
            return ctx.enter_context(nc.psum_tensor(name, [P, 2 * 512], F32))

        def sem(name):
            return ctx.enter_context(nc.semaphore(name))

        table = nc.dram_tensor("table", [NPAD, D], F32, kind="Internal").ap()
        table2 = nc.dram_tensor("table2", [NPAD, ROW2], F32, kind="Internal").ap()

        ident = sb("ident", [P, P])
        ones = sb("ones", [P, P])
        ones_bf = sb("ones_bf", [P, P], BF16)
        neg_ln2 = sb("neg_ln2", [P, P])
        one_dth = sb("one_dth", [P, P])
        win_i = sb("win_i", [P, WIN], I32)
        win = sb("win", [P, WIN])
        pass_i = sb("pass_i", [P, MAX_PASSES], I32)
        pass_at = sb("pass_at", [P, MAX_PASSES])
        offset_i = sb("offset_i", [P, 1], I32)
        neg_offset = sb("neg_offset", [P, 1])

        src_i = sb("src_i", [P, (GROUPS + Q) * CH], I32)
        dst_i = sb("dst_i", [P, GROUPS * CH], I32)
        w_e = sb("w_e", [P, GROUPS * CH])
        c_e = sb("c_e", [P, GROUPS * CH])
        c_t = sb("c_t", [P, GROUPS * CH])
        turns_i = sb("turns_i", [P, GROUPS * CH], I32)
        dst0 = sb("dst0", [P, GROUPS * CH])
        dst_rel = sb("dst_rel", [P, GROUPS * CH])
        least = sb("least", [GROUPS, 1])
        most = sb("most", [GROUPS, 1])
        least_b = sb("least_b", [GROUPS, P])
        span_b = sb("span_b", [GROUPS, P])
        base0 = sb("base0", [P, GROUPS])
        base_f = sb("base_f", [P, GROUPS])
        base_i = sb("base_i", [P, GROUPS], I32)
        span_max = sb("span_max", [P, 1])
        pass_hit = sb("pass_hit", [P, MAX_PASSES])
        passes_f = sb("passes_f", [P, 1])
        passes_i = sb("passes_i", [P, 1], I32)
        basis = sb("basis", [P, TURNS * GROUP])
        staged_src = sb("staged_src", [P, Q, CH], I32)
        rows = sb("rows", [P, Q, CH, ROW2])
        table_rows = rows[:, :, :, :].rearrange("p q j w -> p (q j) w")
        onehot = sb("onehot", [P, 2, CH, WIN], BF16)
        scatter = sb("scatter", [P, 2, CH, WIN])
        gate = sb("gate", [P, CH, WIN])
        work = sb("work", [P, 4, 2, 512])
        slog = work[:, 0, :, :]
        hidden = work[:, 1, :, :]
        filt = work[:, 2, :, :]
        msg = work[:, 3, :, :]
        node_work = work[:, :, :, :].rearrange("p a h e -> p (a h e)")

        pos = sb("pos", [P, NPAD])

        x = sb("x", [P, TILES, D])
        y = sb("y", [P, TILES, D])
        agg = sb("agg", [P, NPAD + WIN])
        deg = sb("deg", [P, NPAD + WIN])
        dst_row = agg[0:GROUPS, 0:GROUP].bitcast(I32)
        score = basis[:, 0:NPAD + WIN]
        deg_col = sb("deg_col", [P, TILES])
        dcol = sb("dcol", [P, TILES])
        stats = sb("stats", [P, TILES, 6])
        mv = sb("mv", [P, TILES, 2])
        neg_mean = sb("neg_mean", [P, TILES])
        var = sb("var", [P, TILES])
        rstd = sb("rstd", [P, TILES])
        newton = sb("newton", [P, TILES])

        w0 = sb("w0", [P, D])
        w3 = sb("w3", [P, D])
        w0T = sb("w0T", [P, D])
        w3T = sb("w3T", [P, D])
        b0 = sb("b0", [P, D])
        b3 = sb("b3", [P, D])
        fw1 = sb("fw1", [P, DEPTH, D])
        fw1_q = sb("fw1_q", [P, Q, D])
        fb1 = sb("fb1", [P, DEPTH])
        fb1_l = sb("fb1_l", [P, 1])
        nfb1 = sb("nfb1", [P, DEPTH])
        nfb1_l = sb("nfb1_l", [P, 1])
        fw2 = sb("fw2", [P, DEPTH, D])
        fb2 = sb("fb2", [P, DEPTH, D])
        lin1 = sb("lin1", [P, DEPTH, D])
        lin2 = sb("lin2", [P, DEPTH, D])
        lb2 = sb("lb2", [P, DEPTH, D])
        ln_g = sb("ln_g", [P, DEPTH, D])
        ln_b = sb("ln_b", [P, DEPTH, D])
        ln_gT = sb("ln_gT", [P, DEPTH])
        ln_bT = sb("ln_bT", [P, DEPTH])
        row_b = sb("row_b", [P, DEPTH, D])
        row_b_l = sb("row_b_l", [P, D])
        gate_w = sb("gate_w", [P, 2])
        gate_wb = sb("gate_wb", [P, P])
        gate_b = sb("gate_b", [P, 1])

        fb1_ln2, lnb_wide, glin = (pos[:, n * DEPTH * D:(n + 1) * DEPTH * D].rearrange("p (l d) -> p l d", d=D)
                                   for n in range(3))

        pA, pB, pC, pD = pb("pA"), pb("pB"), pb("pC"), pb("pD")
        sum_ps = (pC[:, 0:WIN], pC[:, 512:512 + WIN])
        deg_sum_ps = (pD[:, 0:WIN], pD[:, 512:512 + WIN])
        turned_ps = (pA, pB)
        rows_ps = (pC, pD)

        edges_loaded = sem("edges_loaded")
        x_loaded = [sem(f"x_loaded{b}") for b in range(BATCHES)]
        x_pad_set = sem("x_pad_set")
        loaded = sem("loaded")
        pads_set = sem("pads_set")
        pool_own = sem("pool_own")
        consts_made = sem("consts_made")
        dve_own = sem("dve_own")
        act_own = sem("act_own")
        spans_spread = sem("spans_spread")
        windows_ps = sem("windows_ps")
        w_turned = sem("w_turned")
        w_taken = sem("w_taken")
        sums_ps = sem("sums_ps")
        basis_w = sem("basis_w")
        angle_full = sem("angle_full")
        sine_full = sem("sine_full")
        gathers = [sem(f"gathers{q}") for q in range(Q)]
        gathered = [sem(f"gathered{q}") for q in range(Q)]
        staged = [sem(f"staged{q}") for q in range(Q)]
        table_dma = sem("table_dma")
        table_ready = sem("table_ready")
        scatter_full = sem("scatter_full")
        sum_full = sem("sum_full")
        sum_free = sem("sum_free")
        gate_in = sem("gate_in")
        gate_full = sem("gate_full")
        filter_ready = sem("filter_ready")
        bias_ready = sem("bias_ready")
        deg_full = sem("deg_full")
        deg_ps = sem("deg_ps")
        hid_full = [sem(f"hid_full{h}") for h in range(2)]
        slog_full = [sem(f"slog_full{h}") for h in range(2)]
        ssp_full = [sem(f"ssp_full{h}") for h in range(2)]
        filt_full = [sem(f"filt_full{h}") for h in range(2)]
        msg_full = [sem(f"msg_full{h}") for h in range(2)]
        agg_whole = sem("agg_whole")
        stats_made = sem("stats_made")
        abs_full = sem("abs_full")
        mean_full = sem("mean_full")
        centre_in = sem("centre_in")
        centred = sem("centred")
        var_full = sem("var_full")
        guess_full = sem("guess_full")
        rstd_full = sem("rstd_full")
        raw_full = sem("raw_full")
        scaled = sem("scaled")
        tab_full_pool = sem("tab_full_pool")
        normed = sem("normed")
        gained = sem("gained")
        fold_in = sem("fold_in")
        fold_ps = sem("fold_ps")
        log_full = sem("log_full")
        v_full = sem("v_full")
        lin_full = sem("lin_full")
        lin_free = sem("lin_free")
        y_full = sem("y_full")
        yT_ps = sem("yT_ps")
        yT_full = sem("yT_full")
        rows_full = sem("rows_full")
        rows_free = sem("rows_free")
        col_full = sem("col_full")
        score_full = sem("score_full")
        tab_full = sem("tab_full")
        x_done = sem("x_done")
        stored = sem("stored")

        def per_chunk(tile, at):
            return tile[:, bass.ds(at, CH)].unsqueeze(2).broadcast_to([P, CH, WIN])

        def over_chunks(row):
            return row.unsqueeze(1).broadcast_to([P, CH, WIN])

        def over_tiles(row, n):
            return row.unsqueeze(1).broadcast_to([P, n, D])

        def per_tile(col):
            return col.unsqueeze(2).broadcast_to([P, col.shape[1], D])

        def tiles(tile, b):
            return tile[:, cols(b), :]

        def tiles_in(b):
            return range(FIRST[b], FIRST[b] + SIZES[b])

        def cols(b):
            return slice(FIRST[b], FIRST[b] + SIZES[b])

        def as_tiles(ps, b):
            return ps[:, 0:SIZES[b] * P].rearrange("p (k d) -> p k d", d=D)

        def nodes(b):
            return slice(FIRST[b] * P, (FIRST[b] + SIZES[b]) * P)

        def tile_nodes(b, k):
            return slice((FIRST[b] + k) * P, (FIRST[b] + k + 1) * P)

        def table_part(tab, b):
            return tab[nodes(b), :].rearrange("(t p) d -> p t d", p=P)

        def own_of(eng, done):
            def own(ins):
                ins.then_inc(done, 1)
                eng.wait_ge(done, 1)
                eng.sem_inc(done, -1)
            return own

        def statistics(dve, state, b):
            own = own_of(dve, dve_own)
            for t in tiles_in(b):
                ins = dve.bn_stats(stats[:, t, :], state[:, t, :])
            own(ins)
            for t in tiles_in(b):
                ins = dve.bn_aggr(mv[:, t, :], stats[:, t, :])
            return ins

        def inverse_root(dve, root, arg):
            own = own_of(dve, dve_own)
            dve.sem_inc(var_full, 1)
            dve.wait_ge(guess_full, 1)
            dve.sem_inc(guess_full, -1)
            tmp = newton[:, :]
            own(dve.scalar_tensor_tensor(tmp, root, -0.5, root, ALU.mult, ALU.mult))
            own(dve.tensor_tensor(tmp, tmp, arg, ALU.mult))
            own(dve.scalar_tensor_tensor(root, tmp, 1.5, root, ALU.add, ALU.mult))

        def deviations(dve):
            own_of(dve, dve_own)(dve.tensor_scalar(var[:, :], mv[:, :, 1], EPS, None, ALU.add))
            inverse_root(dve, rstd[:, :], var[:, :])

        def guess_power(act, root, arg, power):
            own = own_of(act, act_own)
            act.wait_ge(var_full, 1)
            act.sem_inc(var_full, -1)
            own(act.activation(root, arg, ACT.Ln))
            act.activation(root, root, ACT.Exp, scale=power).then_inc(guess_full, 1)

        def centring_ready(dve, b):
            own = own_of(dve, dve_own)
            own(dve.tensor_scalar(neg_mean[:, cols(b)], mv[:, cols(b), 0], -1.0, None, ALU.mult))
            dve.sem_inc(centre_in, 1)

        def centre_relu(act, dst, b, done):
            act.wait_ge(centre_in, 1)
            act.sem_inc(centre_in, -1)
            for k, t in enumerate(tiles_in(b)):
                ins = act.activation(tiles(dst, b)[:, k, 0:D], x[:, t, :], ACT.Relu, bias=neg_mean[:, t:t + 1])
            ins.then_inc(done, 1)

        def scaled_table(dve):
            for b in range(BATCHES):
                part = tiles(table_rows, b)[:, :, 0:D]
                dve.wait_ge(centred, 1)
                dve.sem_inc(centred, -1)
                dve.tensor_tensor(part, part, per_tile(rstd[:, cols(b)]), ALU.mult).then_inc(tab_full, 1)

        def write_table(act, tab, width, b):
            act.dma_start(table_part(tab, b), tiles(table_rows, b)[:, :, 0:width]).then_inc(table_dma, 16)

        def table_written(act):
            act.wait_ge(table_dma, 16 * BATCHES)
            act.sem_inc(table_dma, -16 * BATCHES)
            act.sem_inc(table_ready, 1)

        def written_by_vector(act, tab, width):
            for b in range(BATCHES):
                act.wait_ge(tab_full, 1)
                act.sem_inc(tab_full, -1)
                write_table(act, tab, width, b)
            table_written(act)

        with nc.Block() as block:

            @block.sync
            def _(sp):
                def load(dst, src, done=edges_loaded):
                    sp.dma_start(dst, src).then_inc(done, 16)

                full = (GROUPS - 1) * GROUP
                sp.wait_ge(pads_set, 1)

                def edges(dst, src):
                    load(dst[:, 0:(GROUPS - 1) * CH].rearrange("p (g j) -> p g j", j=CH),
                         src[0:full].rearrange("(g p j) -> p g j", p=P, j=CH))
                    load(dst[0:LAST_P, (GROUPS - 1) * CH:GROUPS * CH],
                         src[full:full + LAST_P * CH].rearrange("(p j) -> p j", j=CH))
                    load(dst[LAST_P:LAST_P + 1, (GROUPS - 1) * CH:(GROUPS - 1) * CH + LAST_J],
                         src[full + LAST_P * CH:N_EDGES].rearrange("(a j) -> a j", a=1))

                load(dst_row[0:GROUPS - 1, :], a["dst"][0:full].rearrange("(g e) -> g e", e=GROUP))
                load(dst_row[GROUPS - 1:GROUPS, 0:LAST], a["dst"][full:N_EDGES].rearrange("(a e) -> a e", a=1))
                load(dst_row[GROUPS - 1:GROUPS, LAST:GROUP],
                     a["dst"][N_EDGES - (GROUP - LAST):N_EDGES].rearrange("(a e) -> a e", a=1))
                edges(dst_i, a["dst"])
                edges(src_i, a["src"])
                edges(w_e, a["edge_weight"])
                load(src_i[:, GROUPS * CH:(GROUPS + Q) * CH].rearrange("p (g j) -> p g j", j=CH),
                     a["src"][0:Q * GROUP].rearrange("(g p j) -> p g j", p=P, j=CH))
                def load_weight(dst, src, turned=False):
                    sp.dma_start(dst, src, allow_slow_non_contiguous=turned).then_inc(loaded, 16)

                load_weight(w0[:, :], a["L0_gnn_W"])
                load_weight(w3[:, :], a["L3_gnn_W"])
                load_weight(b0[:, :], a["L0_gnn_b"].partition_broadcast(P))
                load_weight(b3[:, :], a["L3_gnn_b"].partition_broadcast(P))
                for q in range(Q):
                    load_weight(fw1[q * RADIAL:(q + 1) * RADIAL, :, :], a["L1_gnn_fw1"].rearrange("l r d -> r l d"))
                load_weight(fb1[:, :], a["L1_gnn_fb1"].rearrange("l d -> d l"), turned=True)
                load_weight(fw2[:, :, :], a["L1_gnn_fw2"].rearrange("l k d -> k l d"))
                load_weight(lin1[:, :, :], a["L1_gnn_lin1_w"].rearrange("l k d -> k l d"))
                load_weight(lin2[:, :, :], a["L1_gnn_lin2_w"].rearrange("l k d -> k l d"))
                for dst, src in ((fb2, "fb2"), (lb2, "lin2_b"), (ln_g, "ln_g"), (ln_b, "ln_b")):
                    load_weight(dst[:, :, :], a["L1_gnn_" + src].partition_broadcast(P))
                load_weight(ln_gT[:, :], a["L1_gnn_ln_g"].rearrange("l d -> d l"), turned=True)
                load_weight(ln_bT[:, :], a["L1_gnn_ln_b"].rearrange("l d -> d l"), turned=True)
                load_weight(gate_w[:, :], a["L2_gnn_gate_w"].rearrange("a (s d) -> d (a s)", d=D), turned=True)
                load_weight(gate_b[:, :], a["L2_gnn_gate_b"].partition_broadcast(P))

            N_EDGE_LOADS = 3 + 9 + 1
            N_LOADS = 4 + Q + 4 + 4 + 4

            @block.scalar
            def _(act):
                act.wait_ge(x_pad_set, 1)
                for b in range(BATCHES):
                    n = SIZES[b] if b < BATCHES - 1 else SIZES[b] - 1
                    act.dma_start(x[:, FIRST[b]:FIRST[b] + n, :],
                                  a["x"][FIRST[b] * P:(FIRST[b] + n) * P, :].rearrange("(t p) d -> p t d", p=P))\
                       .then_inc(x_loaded[b], 16)
                act.dma_start(x[0:TAIL, TILES - 1, :], a["x"][(TILES - 1) * P:N_NODES, :]).then_inc(x_loaded[BATCHES - 1], 16)
                act.preload_act_table_set("natural_log_exp_and_others")
                for b in range(BATCHES):
                    centre_relu(act, table_rows, b, centred)
                guess_power(act, rstd[:, :], var[:, :], -0.5)
                written_by_vector(act, table, D)

            @block.gpsimd
            def _(pool):
                pool.memset(ident[:, :], 0.0).then_inc(pool_own, 1)
                pool.iota(win_i[:, :], pattern=[[1, WIN]], base=0, channel_multiplier=0)
                pool.iota(pass_i[:, :], pattern=[[WIN, MAX_PASSES]], base=0, channel_multiplier=0)
                pool.iota(offset_i[:, :], pattern=[[0, 1]], base=0, channel_multiplier=1)
                pool.wait_ge(pool_own, 1)
                pool.sem_inc(pool_own, -1)
                pool.affine_select(out=ident[:, :], in_=ident[:, :], compare_op=ALU.not_equal, fill=1.0,
                                   base=0, pattern=[[-1, P]], channel_multiplier=1).then_inc(consts_made, 1)

            @block.tensor
            def _(pe):
                pe.wait_ge(spans_spread, 1)
                pe.wait_ge(consts_made, 1)
                pe.matmul(pA[:, 0:GROUPS], least_b[:, :], ident[0:GROUPS, 0:GROUPS], start=True, stop=True)
                pe.matmul(pB[:, 0:GROUPS], span_b[:, :], ident[0:GROUPS, 0:GROUPS], start=True, stop=True)\
                  .then_inc(windows_ps, 1)

            @block.vector
            def _(dve):
                own = own_of(dve, dve_own)

                dve.memset(x[:, TILES - 1, :], 0.0).then_inc(x_pad_set, 1)
                dve.memset(src_i[:, :], 0)
                dve.memset(dst_i[:, :], -1)
                dve.memset(w_e[:, :], 0.0).then_inc(pads_set, 1)
                dve.memset(ones[:, :], 1.0)
                dve.memset(ones_bf[:, :], 1.0)
                dve.memset(neg_ln2[:, :], -LN2)
                dve.memset(one_dth[:, :], 1.0 / D)
                dve.memset(fw1_q[:, :, :], 0.0)
                dve.memset(basis[(Q - 1) * RADIAL:P, (TURNS - 1) * GROUP + LAST:TURNS * GROUP], 0.0)
                dve.memset(deg[:, :], 0.0)
                dve.memset(rows[:, :, :, D:ROW2], 0.0)
                dve.wait_ge(consts_made, 1)
                dve.tensor_copy(win[:, :], win_i[:, :])
                dve.tensor_copy(pass_at[:, :], pass_i[:, :])
                own(dve.tensor_scalar(offset_i[:, :], offset_i[:, :], RADIAL - 1, None, ALU.bitwise_and))
                dve.tensor_scalar(neg_offset[:, :], offset_i[:, :], -CUTOFF / (RADIAL - 1), None, ALU.mult)
                for b in range(BATCHES):
                    dve.wait_ge(x_loaded[b], 16 if b < BATCHES - 1 else 32)
                    own(statistics(dve, x, b))
                    centring_ready(dve, b)
                deviations(dve)
                scaled_table(dve)
                dve.wait_ge(edges_loaded, 16 * N_EDGE_LOADS)
                for q in range(Q):
                    dve.tensor_copy(staged_src[:, q, :], src_i[:, q * CH:(q + 1) * CH])
                dve.tensor_reduce(least[:, :], dst_row[:, :], AX, ALU.min)
                own(dve.tensor_reduce(most[:, :], dst_row[:, :], AX, ALU.max))
                own(dve.tensor_tensor(most[:, :], most[:, :], least[:, :], ALU.subtract))
                dve.tensor_copy(least_b[:, :], least[:, 0:1].broadcast_to([GROUPS, P]))
                dve.tensor_copy(span_b[:, :], most[:, 0:1].broadcast_to([GROUPS, P])).then_inc(spans_spread, 1)
                dve.tensor_copy(dst0[:, :], dst_i[:, :])
                dve.wait_ge(windows_ps, 1)
                dve.tensor_copy(base0[:, :], pA[:, 0:GROUPS])
                own(dve.tensor_reduce(span_max[:, :], pB[:, 0:GROUPS], AX, ALU.max))
                own(dve.tensor_scalar(pass_hit[:, :], pass_at[:, :], span_max[:, 0:1], None, ALU.is_le))
                own(dve.tensor_reduce(passes_f[:, :], pass_hit[:, :], AX, ALU.add))
                dve.tensor_copy(passes_i[:, :], passes_f[:, :])
                dst0_g = dst0[:, :].rearrange("p (g j) -> p g j", j=CH)
                dve.tensor_tensor(dst0_g, dst0_g, base0[:, :].unsqueeze(2).broadcast_to([P, GROUPS, CH]), ALU.subtract)

        with nc.Block() as block:

            @block.sync
            def _(sp):
                n_pass = sp.value_load(passes_i[0:1, 0:1], min_val=1, max_val=MAX_PASSES)
                with sp.Fori(0, n_pass * ((DEPTH + 3) * TURNS)) as n:
                    for q in range(Q):
                        sp.wait_ge(gathers[q], n * (CH * 16) + CH * 16)
                        sp.sem_inc(gathered[q], 1)
                for b in range(BATCHES):
                    sp.wait_ge(x_done, 1)
                    sp.sem_inc(x_done, -1)
                    n = SIZES[b] if b < BATCHES - 1 else SIZES[b] - 1
                    sp.dma_start(out[FIRST[b] * P:(FIRST[b] + n) * P, :].rearrange("(t p) d -> p t d", p=P),
                                 x[:, FIRST[b]:FIRST[b] + n, :]).then_inc(stored, 16)
                sp.dma_start(out[(TILES - 1) * P:N_NODES, :], x[0:TAIL, TILES - 1, :]).then_inc(stored, 16)
                sp.wait_ge(stored, 16 * (BATCHES + 1))


            @block.gpsimd
            def _(pool):
                n_pass = pool.value_load(passes_i[0:1, 0:1], min_val=1, max_val=MAX_PASSES)
                own = own_of(pool, pool_own)

                def gather(tab, width):
                    pool.wait_ge(table_ready, 1)
                    pool.sem_inc(table_ready, -1)
                    with pool.Fori(0, n_pass):
                        with pool.Fori(0, TURNS):
                            for q in range(Q):
                                pool.wait_ge(staged[q], 1)
                                pool.sem_inc(staged[q], -1)
                                for j in range(CH):
                                    pool.indirect_dma_start(
                                        out=rows[:, q, j, 0:width], out_offset=None, in_=tab[:, :],
                                        in_offset=bass.IndirectOffsetOnAxis(ap=staged_src[:, q, j:j + 1], axis=0),
                                    ).then_inc(gathers[q], 16)

                def means():
                    pool.wait_ge(agg_whole, 1)
                    pool.sem_inc(agg_whole, -1)
                    for b in POOL_MEANS:
                        pool.tensor_tensor(pos[:, nodes(b)], agg[:, nodes(b)], deg[:, nodes(b)], ALU.mult).then_inc(mean_full, 1)

                gather(table, D)
                with pool.Fori(0, DEPTH - 1):
                    gather(table, D)
                    means()
                    for b in POOL_BATCHES:
                        pool.wait_ge(scaled, 1)
                        pool.sem_inc(scaled, -1)
                        part = tiles(table_rows, b)[:, :, 0:D]
                        pool.tensor_tensor(part, part, over_tiles(row_b_l[:, :], SIZES[b]), ALU.add).then_inc(tab_full_pool, 1)
                gather(table, D)
                means()
                for b in range(BATCHES):
                    pool.wait_ge(normed, 1)
                    pool.sem_inc(normed, -1)
                    pool.tensor_tensor(tiles(y, b), tiles(y, b), over_tiles(ln_g[:, DEPTH - 1, :], SIZES[b]), ALU.mult).then_inc(gained, 1)
                gather(table2, ROW2)
                gather(table, D)

            @block.tensor
            def _(pe):
                n_pass = pe.value_load(passes_i[0:1, 0:1], min_val=1, max_val=MAX_PASSES)

                def prepare_weights():
                    pe.wait_ge(loaded, 16 * N_LOADS)
                    pe.transpose(pA[:, 0:P], w0[:, :], ident[:, :])
                    pe.transpose(pB[:, 0:P], w3[:, :], ident[:, :]).then_inc(w_turned, 1)
                    pe.wait_ge(w_taken, 1)
                    pe.sem_inc(w_taken, -1)
                    for l in range(DEPTH):
                        pe.matmul(pA[:, l * D:(l + 1) * D], fb1_ln2[:, l, :], fw2[:, l, :], start=True, stop=True)
                        last = pe.matmul(pB[:, l * D:(l + 1) * D], neg_ln2[:, :], lin2[:, l, :], start=True, stop=True)
                    last.then_inc(sums_ps, 1)
                    pe.wait_ge(fold_in, 1)
                    pe.sem_inc(fold_in, -1)
                    for l in range(1, DEPTH):
                        pe.matmul(pA[:, l * D:(l + 1) * D], lnb_wide[:, l, :], lin1[:, l, :], start=True, stop=True)
                        last = pe.matmul(pB[:, l * D:(l + 1) * D], one_dth[:, :], glin[:, l, :], start=True, stop=True)
                    last.then_inc(fold_ps, 1)

                def plain_edges(degrees=False):
                    with pe.Fori(0, n_pass):
                        with pe.Fori(0, TURNS):
                            for q in range(Q):
                                pe.wait_ge(scatter_full, 1)
                                pe.sem_inc(scatter_full, -1)
                                pe.wait_ge(sum_free, 1)
                                pe.sem_inc(sum_free, -1)
                                if degrees:
                                    for j in range(CH):
                                        pe.matmul(deg_sum_ps[q % 2], ones_bf[:, :], onehot[:, q % 2, j, :],
                                                  start=(j == 0), stop=(j == CH - 1))
                                for j in range(CH):
                                    mm = pe.matmul(sum_ps[q % 2], rows[:, q, j, 0:D], scatter[:, q % 2, j, :],
                                                   start=(j == 0), stop=(j == CH - 1))
                                mm.then_inc(sum_full, 1)

                def hidden_units(i, q, h):
                    pe.matmul(pA[:, h * 512:(h + 1) * 512], fw1_q[:, q, :],
                              basis[:, bass.ds(i * GROUP + h, 512, 2)], start=True, stop=True).then_inc(hid_full[h], 1)

                def conv_turn(l, i, last):
                    for q in range(Q):
                        for h in range(2):
                            pe.wait_ge(ssp_full[h], 1)
                            pe.sem_inc(ssp_full[h], -1)
                            for c in range(CH // 2):
                                mm = pe.matmul(pB[:, h * 512 + c * D:h * 512 + (c + 1) * D],
                                               hidden[:, h, c:512:CH // 2], fw2[:, l, :], start=True, stop=True)
                            mm.then_inc(filt_full[h], 1)
                            if q < Q - 1:
                                hidden_units(i, q + 1, h)
                            elif not last:
                                hidden_units(i + 1, 0, h)
                        pe.wait_ge(scatter_full, 1)
                        pe.sem_inc(scatter_full, -1)
                        pe.wait_ge(sum_free, 1)
                        pe.sem_inc(sum_free, -1)
                        for h in range(2):
                            pe.wait_ge(msg_full[h], 1)
                            pe.sem_inc(msg_full[h], -1)
                            for c in range(CH // 2):
                                mm = pe.matmul(sum_ps[q % 2], msg[:, h, c * D:(c + 1) * D], scatter[:, q % 2, 2 * c + h, :],
                                               start=(h == 0 and c == 0), stop=(h == 1 and c == CH // 2 - 1))
                        mm.then_inc(sum_full, 1)

                def conv_edges(l):
                    pe.wait_ge(filter_ready, 1)
                    pe.sem_inc(filter_ready, -1)
                    with pe.Fori(0, n_pass):
                        for h in range(2):
                            hidden_units(0, 0, h)
                        with pe.Fori(0, TURNS - 1) as i:
                            conv_turn(l, i, last=False)
                        conv_turn(l, TURNS - 1, last=True)

                def linear(weights, ready=None):
                    for b in range(BATCHES):
                        if ready is not None:
                            pe.wait_ge(ready, 1)
                            pe.sem_inc(ready, -1)
                        if b >= 2:
                            pe.wait_ge(lin_free, 1)
                            pe.sem_inc(lin_free, -1)
                        ps = turned_ps[b % 2]
                        for k in range(SIZES[b]):
                            to, at = ps[:, k * D:(k + 1) * D], agg[:, tile_nodes(b, k)]
                            mm = pe.transpose(to, at, ident[:, :]) if weights is None else \
                                pe.matmul(to, at, weights, start=True, stop=True)
                        mm.then_inc(lin_full, 1)

                def linear_and_rows(weights, ready, row_weights):
                    def lin(s):
                        if ready is not None:
                            pe.wait_ge(ready, 1)
                            pe.sem_inc(ready, -1)
                        if s >= 2:
                            pe.wait_ge(lin_free, 1)
                            pe.sem_inc(lin_free, -1)
                        for k in range(SIZES[s]):
                            mm = pe.matmul(turned_ps[s % 2][:, k * D:(k + 1) * D], agg[:, tile_nodes(s, k)], weights,
                                           start=True, stop=True)
                        mm.then_inc(lin_full, 1)

                    lin(0)
                    lin(1)
                    for s in range(1, BATCHES + 2):
                        if s + 1 < BATCHES and ready is None:
                            lin(s + 1)
                        if s >= 2:
                            pe.wait_ge(yT_full, 1)
                            pe.sem_inc(yT_full, -1)
                        if s <= BATCHES:
                            pe.wait_ge(y_full, 1)
                            pe.sem_inc(y_full, -1)
                            for k in range(SIZES[s - 1]):
                                mm = pe.transpose(pC[:, k * P:(k + 1) * P], y[:, FIRST[s - 1] + k, :], ident[:, :])
                            mm.then_inc(yT_ps, 1)
                        if s >= 2:
                            if s >= 3:
                                pe.wait_ge(rows_free, 1)
                                pe.sem_inc(rows_free, -1)
                            for k in range(SIZES[s - 2]):
                                mm = pe.matmul(pD[:, k * D:(k + 1) * D], node_work[:, tile_nodes(s - 2, k)], row_weights,
                                               start=True, stop=True)
                            mm.then_inc(rows_full, 1)
                        if s + 1 < BATCHES and ready is not None:
                            lin(s + 1)
                    pe.wait_ge(lin_free, 2)
                    pe.sem_inc(lin_free, -2)
                    pe.wait_ge(rows_free, 1)
                    pe.sem_inc(rows_free, -1)

                def through_turned(use):
                    for b in range(BATCHES + 1):
                        if b < BATCHES:
                            pe.wait_ge(y_full, 1)
                            pe.sem_inc(y_full, -1)
                            for k in range(SIZES[b]):
                                mm = pe.transpose(turned_ps[b % 2][:, k * P:(k + 1) * P], y[:, FIRST[b] + k, :], ident[:, :])
                            mm.then_inc(yT_ps, 1)
                        if b >= 1:
                            pe.wait_ge(yT_full, 1)
                            pe.sem_inc(yT_full, -1)
                            use(b - 1)

                prepare_weights()
                plain_edges(degrees=True)
                pe.wait_ge(deg_full, 1)
                pe.sem_inc(deg_full, -1)
                linear_and_rows(w0T[:, :], None, lin1[:, 0, :])
                for t in range(TILES):
                    mm = pe.matmul(pD[:, t:t + 1], deg[0:1, t * P:(t + 1) * P], ones[0:1, 0:1], start=True, stop=True)
                mm.then_inc(deg_ps, 1)
                with pe.Fori(0, DEPTH - 1) as l:
                    conv_edges(l)
                    linear_and_rows(lin2[:, l, :], v_full, lin1[:, l + 1, :])
                conv_edges(DEPTH - 1)
                linear(lin2[:, DEPTH - 1, :], v_full)
                pe.wait_ge(lin_free, 2)
                pe.sem_inc(lin_free, -2)

                def source_scores(b):
                    if b >= 2:
                        pe.wait_ge(rows_free, 1)
                        pe.sem_inc(rows_free, -1)
                    for k in range(SIZES[b]):
                        mm = pe.matmul(rows_ps[b % 2][:, k:k + 1], node_work[:, tile_nodes(b, k)], gate_w[:, 1:2],
                                       start=True, stop=True)
                    mm.then_inc(col_full, 1)

                through_turned(source_scores)
                pe.wait_ge(rows_free, 2)
                pe.sem_inc(rows_free, -2)
                for b in range(BATCHES):
                    if b >= 2:
                        pe.wait_ge(rows_free, 1)
                        pe.sem_inc(rows_free, -1)
                    yT, ps = node_work[:, nodes(b)], rows_ps[b % 2]
                    n = SIZES[b] * P
                    for at in range(0, n, 512):
                        mm = pe.matmul(ps[:, at:min(at + 512, n)], gate_wb[:, :], yT[:, at:min(at + 512, n)],
                                       start=True, stop=True)
                    mm.then_inc(rows_full, 1)
                pe.wait_ge(rows_free, 2)
                pe.sem_inc(rows_free, -2)
                plain_edges()
                linear(None)
                pe.wait_ge(lin_free, 2)
                pe.sem_inc(lin_free, -2)
                plain_edges()
                linear(w3T[:, :])
                pe.wait_ge(lin_free, 2)
                pe.sem_inc(lin_free, -2)

            @block.scalar
            def _(act):
                n_pass = act.value_load(passes_i[0:1, 0:1], min_val=1, max_val=MAX_PASSES)

                def own(ins):
                    ins.then_inc(act_own, 1)
                    act.wait_ge(act_own, 1)
                    act.sem_inc(act_own, -1)

                def basis_of_edges():
                    for q in range(Q):
                        n = TURNS if q < Q - 1 else TURNS - 1
                        act.dma_start(
                            basis[q * RADIAL:(q + 1) * RADIAL, 0:n * GROUP].rearrange("r (i e) -> r i e", e=GROUP),
                            a["edge_weight"][0:(GROUPS - 1) * GROUP]
                            .rearrange("(i s e) -> i s e", s=1, e=GROUP)[q:(n - 1) * Q + q + 1:Q, 0, :]
                            .partition_broadcast(RADIAL)).then_inc(basis_w, 16)
                    act.dma_start(basis[(Q - 1) * RADIAL:P, (TURNS - 1) * GROUP:(TURNS - 1) * GROUP + LAST],
                                  a["edge_weight"][(GROUPS - 1) * GROUP:N_EDGES].partition_broadcast(RADIAL))\
                       .then_inc(basis_w, 16)
                    act.wait_ge(angle_full, 1)
                    act.sem_inc(angle_full, -1)
                    act.activation(c_t[:, :], c_e[:, :], ACT.Sin, scale=math.pi / (2 * CUTOFF)).then_inc(sine_full, 1)
                    act.preload_act_table_set("natural_log_exp_and_others")
                    act.wait_ge(basis_w, 16 * (Q + 1))
                    own(act.activation(basis[:, :], basis[:, :], ACT.Square, bias=neg_offset[:, 0:1]))
                    step = CUTOFF / (RADIAL - 1)
                    own(act.activation(basis[:, :], basis[:, :], ACT.Exp, scale=-0.5 / (step * step)))

                def softplus_log(dst, arg, full, **bias):
                    own(act.activation(dst, arg, ACT.Abs, **bias))
                    own(act.activation(dst, dst, ACT.Exp, scale=-1.0))
                    act.activation(dst, dst, ACT.Ln, bias=1.0).then_inc(full, 1)

                def turned(b, ps):
                    act.wait_ge(yT_ps, 1)
                    act.sem_inc(yT_ps, -1)
                    act.activation(node_work[:, nodes(b)], ps[:, 0:SIZES[b] * P], ACT.Copy).then_inc(yT_full, 1)

                def next_table(maps):
                    lag = 2 if maps else 1
                    for s in range(BATCHES + lag + 1):
                        if s < BATCHES and maps:
                            act.wait_ge(abs_full, 1)
                            act.sem_inc(abs_full, -1)
                            own(act.activation(node_work[:, nodes(s)], node_work[:, nodes(s)], ACT.Exp, scale=-1.0))
                            act.activation(node_work[:, nodes(s)], node_work[:, nodes(s)], ACT.Ln, bias=1.0)\
                               .then_inc(log_full, 1)
                        if s < BATCHES and not maps:
                            centre_relu(act, y, s, y_full)
                        if lag <= s < BATCHES + lag:
                            turned(s - lag, pC)
                        if s == BATCHES + lag - 1:
                            guess_power(act, rstd[:, :], var[:, :], -0.5)
                        if s > lag:
                            b = s - lag - 1
                            act.wait_ge(rows_full, 1)
                            act.sem_inc(rows_full, -1)
                            own(act.activation(tiles(table_rows, b)[:, :, 0:D], as_tiles(pD, b), ACT.Copy))
                            act.sem_inc(rows_free, 1)
                            if not (maps and b in POOL_BATCHES):
                                act.sem_inc(raw_full, 1)
                    if maps:
                        act.wait_ge(rstd_full, 1)
                        act.sem_inc(rstd_full, -1)
                        for b in POOL_BATCHES:
                            for k, t in enumerate(tiles_in(b)):
                                ins = act.activation(table_rows[:, t, 0:D], table_rows[:, t, 0:D], ACT.Copy,
                                                     scale=rstd[:, t:t + 1])
                            ins.then_inc(scaled, 1)
                    for b in range(BATCHES):
                        if maps and b in POOL_BATCHES:
                            act.wait_ge(tab_full_pool, 1)
                            act.sem_inc(tab_full_pool, -1)
                        else:
                            act.wait_ge(tab_full, 1)
                            act.sem_inc(tab_full, -1)
                        write_table(act, table, D, b)
                    table_written(act)

                def conv_edges():
                    act.wait_ge(bias_ready, 1)
                    act.sem_inc(bias_ready, -1)
                    with act.Fori(0, n_pass):
                        with act.Fori(0, TURNS):
                            for q in range(Q):
                                for h in range(2):
                                    act.wait_ge(hid_full[h], 1)
                                    act.sem_inc(hid_full[h], -1)
                                    softplus_log(slog[:, h, :], pA[:, h * 512:(h + 1) * 512], slog_full[h],
                                                 bias=fb1_l[:, 0:1])

                basis_of_edges()
                next_table(maps=False)
                guess_power(act, dcol[:, :], deg_col[:, :], -0.5)
                guess_power(act, pos[:, :], deg[:, 0:NPAD], -1.0)
                with act.Fori(0, DEPTH - 1):
                    conv_edges()
                    next_table(maps=True)
                conv_edges()
                for b in range(BATCHES):
                    act.wait_ge(abs_full, 1)
                    act.sem_inc(abs_full, -1)
                    own(act.activation(node_work[:, nodes(b)], node_work[:, nodes(b)], ACT.Exp, scale=-1.0))
                    act.activation(node_work[:, nodes(b)], node_work[:, nodes(b)], ACT.Ln, bias=1.0).then_inc(log_full, 1)
                guess_power(act, rstd[:, :], var[:, :], -0.5)
                act.wait_ge(rstd_full, 1)
                act.sem_inc(rstd_full, -1)
                for b in range(BATCHES):
                    for k, t in enumerate(tiles_in(b)):
                        ins = act.activation(y[:, t, :], y[:, t, :], ACT.Identity, bias=neg_mean[:, t:t + 1],
                                             scale=rstd[:, t:t + 1])
                    ins.then_inc(normed, 1)
                for b in range(BATCHES):
                    centre_relu(act, y, b, centred)
                guess_power(act, rstd[:, :], var[:, :], -0.5)
                for b in range(BATCHES + 1):
                    if b < BATCHES:
                        turned(b, turned_ps[b % 2])
                    if b >= 1:
                        act.wait_ge(tab_full, 1)
                        act.sem_inc(tab_full, -1)
                        act.sem_inc(rows_free, 1)
                        write_table(act, table2, ROW2, b - 1)
                table_written(act)
                for b in range(BATCHES):
                    act.wait_ge(rows_full, 1)
                    act.sem_inc(rows_full, -1)
                    own(act.activation(score[:, nodes(b)], rows_ps[b % 2][:, 0:SIZES[b] * P], ACT.Copy))
                    act.sem_inc(rows_free, 1)
                act.sem_inc(score_full, 1)
                with act.Fori(0, n_pass):
                    with act.Fori(0, TURNS):
                        for q in range(Q):
                            act.wait_ge(gate_in, 1)
                            act.sem_inc(gate_in, -1)
                            act.activation(gate[:, :, :], gate[:, :, :], ACT.Tanh).then_inc(gate_full, 1)
                act.preload_act_table_set("natural_log_exp_and_others")
                for b in range(BATCHES):
                    centre_relu(act, table_rows, b, centred)
                guess_power(act, rstd[:, :], var[:, :], -0.5)
                written_by_vector(act, table, D)

            @block.vector
            def _(dve):
                n_pass = dve.value_load(passes_i[0:1, 0:1], min_val=1, max_val=MAX_PASSES)

                def own(ins):
                    ins.then_inc(dve_own, 1)
                    dve.wait_ge(dve_own, 1)
                    dve.sem_inc(dve_own, -1)

                for q in range(Q):
                    dve.sem_inc(staged[q], 1)
                dve.sem_inc(sum_free, 2)

                def prepare_weights():
                    own(dve.tensor_scalar(turns_i[:, :], w_e[:, :], 1.0 / (2 * CUTOFF), None, ALU.mult))
                    own(dve.scalar_tensor_tensor(c_e[:, :], turns_i[:, :], -2 * CUTOFF, w_e[:, :], ALU.mult, ALU.add))
                    dve.sem_inc(angle_full, 1)
                    dve.wait_ge(loaded, 16 * N_LOADS)
                    dve.tensor_scalar(nfb1[:, :], fb1[:, :], -1.0, None, ALU.mult)
                    dve.tensor_scalar(fb1_ln2[:, :, :], fb1[:, :].unsqueeze(2).broadcast_to([P, DEPTH, P]), -LN2, None,
                                      ALU.add)
                    dve.tensor_copy(gate_wb[:, :], gate_w[:, 0:1].broadcast_to([P, P]))
                    dve.wait_ge(w_turned, 1)
                    dve.sem_inc(w_turned, -1)
                    dve.tensor_copy(w0T[:, :], pA[:, 0:P])
                    dve.tensor_copy(w3T[:, :], pB[:, 0:P]).then_inc(w_taken, 1)
                    dve.wait_ge(sine_full, 1)
                    dve.sem_inc(sine_full, -1)
                    own(dve.tensor_tensor(c_t[:, :], c_t[:, :], c_t[:, :], ALU.mult))
                    own(dve.tensor_scalar(c_t[:, :], c_t[:, :], -1.0, 1.0, ALU.mult, ALU.add))
                    own(dve.tensor_scalar(c_e[:, :], w_e[:, :], CUTOFF, None, ALU.is_lt))
                    dve.tensor_tensor(c_e[:, :], c_e[:, :], c_t[:, :], ALU.mult)
                    dve.wait_ge(sums_ps, 1)
                    dve.sem_inc(sums_ps, -1)
                    for bias, ps in ((fb2, pA), (lb2, pB)):
                        flat = bias[:, :, :].rearrange("p l d -> p (l d)")
                        ins = dve.tensor_tensor(flat, flat, ps[:, 0:DEPTH * D], ALU.add)
                    own(ins)
                    for l in range(1, DEPTH):
                        dve.tensor_scalar(glin[:, l, :], lin1[:, l, :], ln_gT[:, l - 1:l], None, ALU.mult)
                    own(dve.tensor_copy(lnb_wide[:, 1:DEPTH, :],
                                        ln_bT[:, 0:DEPTH - 1].unsqueeze(2).broadcast_to([P, DEPTH - 1, P])))
                    dve.sem_inc(fold_in, 1)
                    dve.wait_ge(fold_ps, 1)
                    dve.sem_inc(fold_ps, -1)

                    def flat(tile, first, end):
                        return tile[:, first:end, :].rearrange("p l d -> p (l d)")
                    dve.tensor_copy(flat(row_b, 1, DEPTH), pA[:, D:DEPTH * D])
                    dve.tensor_tensor(flat(lin1, 1, DEPTH), flat(glin, 1, DEPTH), pB[:, D:DEPTH * D], ALU.subtract)
                    own(dve.tensor_tensor(flat(lb2, 1, DEPTH), flat(lb2, 1, DEPTH), flat(ln_b, 0, DEPTH - 1), ALU.add))

                def start_sums():
                    dve.memset(agg[:, :], 0.0)
                    dve.tensor_copy(dst_rel[:, :], dst0[:, :])
                    dve.tensor_copy(base_f[:, :], base0[:, :])
                    own(dve.tensor_copy(base_i[:, :], base0[:, :]))

                def next_pass():
                    dve.tensor_scalar(dst_rel[:, :], dst_rel[:, :], -float(WIN), None, ALU.add)
                    own(dve.tensor_scalar(base_f[:, :], base_f[:, :], float(WIN), float(NPAD), ALU.add, ALU.min))
                    own(dve.tensor_copy(base_i[:, :], base_f[:, :]))

                def window_start(i, q):
                    return dve.value_load(base_i[0:1, bass.ds(i * Q + q, 1)], min_val=0, max_val=NPAD)

                def match(dst, at):
                    return dve.tensor_tensor(dst, over_chunks(win[:, :]), per_chunk(dst_rel, at), ALU.is_equal)

                def add_sums(i, q, base, degrees=False):
                    dve.wait_ge(sum_full, 1)
                    dve.sem_inc(sum_full, -1)
                    dve.tensor_copy(staged_src[:, q, :], src_i[:, bass.ds(i * (Q * CH) + (Q + q) * CH, CH)])\
                       .then_inc(staged[q], 1)
                    if degrees:
                        dve.tensor_tensor(deg[:, bass.ds(base, WIN)], deg[:, bass.ds(base, WIN)], deg_sum_ps[q % 2], ALU.add)
                    own(dve.tensor_tensor(agg[:, bass.ds(base, WIN)], agg[:, bass.ds(base, WIN)], sum_ps[q % 2], ALU.add))
                    dve.sem_inc(sum_free, 1)

                def last_sum():
                    dve.wait_ge(sum_free, 2)

                def plain_edges(kind):
                    def begin(i, q):
                        at = i * (Q * CH) + q * CH
                        pair, factors = onehot[:, q % 2, :, :], per_chunk(w_e, at)
                        dve.wait_ge(gathered[q], 1)
                        dve.sem_inc(gathered[q], -1)
                        if kind == "count":
                            match(scatter[:, q % 2, :, :], at).then_inc(scatter_full, 1)
                        elif kind == "weight":
                            own(match(pair, at))
                            dve.tensor_tensor(scatter[:, q % 2, :, :], pair, factors, ALU.mult).then_inc(scatter_full, 1)
                        else:
                            dve.tensor_tensor(gate[:, :, :], over_chunks(score[:, bass.ds(window_start(i, q), WIN)]),
                                              rows[:, q, :, D:D + 1].broadcast_to([P, CH, WIN]), ALU.add)\
                               .then_inc(gate_in, 1)
                            own(match(pair, at))
                            own(dve.tensor_tensor(scatter[:, q % 2, :, :], pair, factors, ALU.mult))

                    def finish(q):
                        if kind == "gate":
                            dve.wait_ge(gate_full, 1)
                            dve.sem_inc(gate_full, -1)
                            part = scatter[:, q % 2, :, :]
                            own(dve.tensor_tensor(part, part, gate[:, :, :], ALU.mult))
                            dve.sem_inc(scatter_full, 1)

                    def turn(i, last):
                        for q in range(Q):
                            if q < Q - 1:
                                begin(i, q + 1)
                            elif not last:
                                begin(i + 1, 0)
                            add_sums(i, q, window_start(i, q), degrees=(kind == "weight"))
                            if not (last and q == Q - 1):
                                finish((q + 1) % Q)

                    with dve.Fori(0, n_pass):
                        begin(0, 0)
                        finish(0)
                        with dve.Fori(0, TURNS - 1) as i:
                            turn(i, last=False)
                        turn(TURNS - 1, last=True)
                        next_pass()
                    last_sum()

                def softplus_rest(h):
                    dve.wait_ge(slog_full[h], 1)
                    dve.sem_inc(slog_full[h], -1)
                    dve.scalar_tensor_tensor(hidden[:, h, :], pA[:, h * 512:(h + 1) * 512], nfb1_l[:, 0:1],
                                             slog[:, h, :], ALU.max, ALU.add).then_inc(ssp_full[h], 1)

                def conv_scatter(i, q):
                    at = i * (Q * CH) + q * CH
                    own(match(onehot[:, q % 2, :, :], at))
                    dve.tensor_tensor(scatter[:, q % 2, :, :], onehot[:, q % 2, :, :], per_chunk(c_e, at), ALU.mult)\
                       .then_inc(scatter_full, 1)

                def conv_turn(l, i, last):
                    for q in range(Q):
                        for h in range(2):
                            dve.wait_ge(filt_full[h], 1)
                            dve.sem_inc(filt_full[h], -1)
                            ins = dve.tensor_tensor(
                                filt[:, h, :].rearrange("p (c d) -> p c d", d=D),
                                pB[:, h * 512:(h + 1) * 512].rearrange("p (c d) -> p c d", d=D),
                                over_tiles(fb2[:, l, :], CH // 2), ALU.add)
                        own(ins)
                        dve.wait_ge(gathered[q], 1)
                        dve.sem_inc(gathered[q], -1)
                        for h in range(2):
                            dve.tensor_tensor(msg[:, h, :].rearrange("p (c d) -> p c d", d=D),
                                              filt[:, h, :].rearrange("p (c d) -> p c d", d=D),
                                              rows[:, q, h:CH:2, 0:D], ALU.mult).then_inc(msg_full[h], 1)
                        if not (last and q == Q - 1):
                            for h in range(2):
                                softplus_rest(h)
                            if q < Q - 1:
                                conv_scatter(i, q + 1)
                            else:
                                conv_scatter(i + 1, 0)
                        add_sums(i, q, window_start(i, q))

                def conv_edges(l, last):
                    for q in range(Q):
                        dve.tensor_copy(fw1_q[q * RADIAL:(q + 1) * RADIAL, q, :], fw1[q * RADIAL:(q + 1) * RADIAL, l, :])
                    dve.tensor_copy(nfb1_l[:, :], nfb1[:, bass.ds(l, 1)]).then_inc(filter_ready, 1)
                    own(dve.tensor_copy(fb1_l[:, :], fb1[:, bass.ds(l, 1)]))
                    dve.sem_inc(bias_ready, 1)
                    start_sums()
                    if not last:
                        dve.wait_ge(gathered[0], 1)
                        own(dve.tensor_copy(row_b_l[:, :], row_b[:, l + 1, :]))
                    with dve.Fori(0, n_pass):
                        for h in range(2):
                            softplus_rest(h)
                        conv_scatter(0, 0)
                        with dve.Fori(0, TURNS - 1) as i:
                            conv_turn(l, i, last=False)
                        conv_turn(l, TURNS - 1, last=True)
                        next_pass()
                    last_sum()

                def over_nodes(tile):
                    return tile[:, :].unsqueeze(2).broadcast_to([P, TILES, D])

                start_sums()
                prepare_weights()
                dve.tensor_tensor(x[:, :, :], x[:, :, :], over_tiles(b0[:, :], TILES), ALU.add)
                plain_edges("weight")
                dve.sem_inc(deg_full, 1)
                for b in range(BATCHES):
                    dve.wait_ge(lin_full, 1)
                    dve.sem_inc(lin_full, -1)
                    own(dve.tensor_tensor(tiles(x, b), as_tiles(turned_ps[b % 2], b), tiles(x, b), ALU.add))
                    dve.sem_inc(lin_free, 1)
                    own(statistics(dve, x, b))
                    centring_ready(dve, b)
                deviations(dve)
                dve.wait_ge(raw_full, BATCHES)
                dve.sem_inc(raw_full, -BATCHES)
                for b in range(BATCHES):
                    part = tiles(table_rows, b)[:, :, 0:D]
                    dve.tensor_tensor(part, part, per_tile(rstd[:, cols(b)]), ALU.mult).then_inc(tab_full, 1)
                own(dve.tensor_tensor(y[:, :, :], y[:, :, :], over_nodes(rstd), ALU.mult))
                own(dve.tensor_tensor(y[:, :, :], y[:, :, :], over_tiles(lb2[:, 0, :], TILES), ALU.add))
                dve.wait_ge(deg_ps, 1)
                dve.sem_inc(deg_ps, -1)
                own(dve.tensor_scalar(deg_col[:, :], pD[:, 0:TILES], 1.0, None, ALU.max))
                inverse_root(dve, dcol[:, :], deg_col[:, :])
                own(dve.tensor_scalar(deg[:, :], deg[:, :], 1.0, None, ALU.max))
                dve.sem_inc(var_full, 1)
                dve.wait_ge(guess_full, 1)
                dve.sem_inc(guess_full, -1)
                own(dve.scalar_tensor_tensor(node_work[:, 0:NPAD], deg[:, 0:NPAD], -1.0, pos[:, :], ALU.mult, ALU.mult))
                own(dve.scalar_tensor_tensor(deg[:, 0:NPAD], node_work[:, 0:NPAD], 2.0, pos[:, :], ALU.add, ALU.mult))

                def conv_layer(l, last):
                    conv_edges(l, last)
                    dve.sem_inc(agg_whole, 1)

                    def absolute(b):
                        if b in POOL_MEANS:
                            dve.wait_ge(mean_full, 1)
                            dve.sem_inc(mean_full, -1)
                        else:
                            own(dve.tensor_tensor(pos[:, nodes(b)], agg[:, nodes(b)], deg[:, nodes(b)], ALU.mult))
                        dve.scalar_tensor_tensor(node_work[:, nodes(b)], pos[:, nodes(b)], -1.0, pos[:, nodes(b)],
                                                 ALU.mult, ALU.max).then_inc(abs_full, 1)

                    def aggregate(b):
                        dve.wait_ge(stats_made, 1)
                        dve.sem_inc(stats_made, -1)
                        for t in tiles_in(b):
                            ins = dve.bn_aggr(mv[:, t, :], stats[:, t, :])
                        return ins

                    absolute(0)
                    absolute(1)
                    for s in range(BATCHES + 1):
                        if s < BATCHES:
                            dve.wait_ge(log_full, 1)
                            dve.sem_inc(log_full, -1)
                            dve.scalar_tensor_tensor(agg[:, nodes(s)], pos[:, nodes(s)], 0.0, node_work[:, nodes(s)],
                                                     ALU.max, ALU.add).then_inc(v_full, 1)
                        if s + 2 < BATCHES:
                            absolute(s + 2)
                        if s >= 1:
                            b = s - 1
                            dve.wait_ge(lin_full, 1)
                            dve.sem_inc(lin_full, -1)
                            dve.tensor_tensor(tiles(y, b), as_tiles(turned_ps[b % 2], b), tiles(y, b), ALU.add)\
                               .then_inc(dve_own, 1)
                            if b >= 1:
                                aggregate(b - 1)
                            dve.wait_ge(dve_own, 1)
                            dve.sem_inc(dve_own, -1)
                            dve.sem_inc(lin_free, 1)
                            if not last:
                                dve.sem_inc(y_full, 1)
                            for t in tiles_in(b):
                                ins = dve.bn_stats(stats[:, t, :], y[:, t, :])
                            ins.then_inc(stats_made, 1)
                    own(aggregate(BATCHES - 1))
                    deviations(dve)
                    if last:
                        own(dve.scalar_tensor_tensor(neg_mean[:, :], mv[:, :, 0], -1.0, rstd[:, :], ALU.mult, ALU.mult))
                        dve.sem_inc(rstd_full, 1)
                        return
                    dve.sem_inc(rstd_full, 1)
                    for b in range(BATCHES):
                        if b in POOL_BATCHES:
                            continue
                        dve.wait_ge(raw_full, 1)
                        dve.sem_inc(raw_full, -1)
                        for k, t in enumerate(tiles_in(b)):
                            row = table_rows[:, t, 0:D]
                            ins = dve.scalar_tensor_tensor(row, row, rstd[:, t:t + 1], row_b_l[:, :], ALU.mult, ALU.add)
                        ins.then_inc(tab_full, 1)
                    own(dve.tensor_tensor(y[:, :, :], y[:, :, :], mv[:, :, 0:1].broadcast_to([P, TILES, D]), ALU.subtract))
                    own(dve.tensor_tensor(y[:, :, :], y[:, :, :], over_nodes(rstd), ALU.mult))
                    own(dve.tensor_tensor(y[:, :, :], y[:, :, :], over_tiles(ln_g[:, l, :], TILES), ALU.mult))
                    own(dve.tensor_tensor(y[:, :, :], y[:, :, :], over_tiles(lb2[:, l + 1, :], TILES), ALU.add))

                with dve.Fori(0, DEPTH - 1) as l:
                    conv_layer(l, last=False)
                dve.tensor_tensor(x[:, :, :], x[:, :, :], over_tiles(ln_b[:, DEPTH - 1, :], TILES), ALU.add)
                conv_layer(DEPTH - 1, last=True)

                own(dve.memset(score[:, NPAD:NPAD + WIN], 0.0))
                for b in range(BATCHES):
                    dve.wait_ge(gained, 1)
                    dve.sem_inc(gained, -1)
                    own(dve.tensor_tensor(tiles(x, b), tiles(x, b), tiles(y, b), ALU.add))
                    own(statistics(dve, x, b))
                    centring_ready(dve, b)
                deviations(dve)
                for b in range(BATCHES):
                    dve.wait_ge(centred, 1)
                    dve.sem_inc(centred, -1)
                    own(dve.tensor_tensor(tiles(y, b), tiles(y, b), per_tile(rstd[:, cols(b)]), ALU.mult))
                    dve.sem_inc(y_full, 1)
                for b in range(BATCHES):
                    part = tiles(table_rows, b)
                    own(dve.tensor_tensor(part[:, :, 0:D], tiles(y, b), per_tile(dcol[:, cols(b)]), ALU.mult))
                    dve.wait_ge(col_full, 1)
                    dve.sem_inc(col_full, -1)
                    dve.tensor_scalar(part[:, :, D:D + 1], rows_ps[b % 2][:, 0:SIZES[b]].unsqueeze(2), gate_b[:, 0:1], None,
                                      ALU.add).then_inc(tab_full, 1)
                start_sums()
                dve.wait_ge(score_full, 1)
                dve.sem_inc(score_full, -1)
                plain_edges("gate")
                for b in range(BATCHES):
                    dve.wait_ge(lin_full, 1)
                    dve.sem_inc(lin_full, -1)
                    for k, t in enumerate(tiles_in(b)):
                        ins = dve.scalar_tensor_tensor(x[:, t, :], turned_ps[b % 2][:, k * D:(k + 1) * D], dcol[:, t:t + 1],
                                                       x[:, t, :], ALU.mult, ALU.add)
                    own(ins)
                    dve.sem_inc(lin_free, 1)
                    own(statistics(dve, x, b))
                    centring_ready(dve, b)
                deviations(dve)
                scaled_table(dve)

                start_sums()
                dve.tensor_tensor(x[:, :, :], x[:, :, :], over_tiles(b3[:, :], TILES), ALU.add)
                plain_edges("count")
                for b in range(BATCHES):
                    dve.wait_ge(lin_full, 1)
                    dve.sem_inc(lin_full, -1)
                    own(dve.tensor_tensor(tiles(x, b), as_tiles(turned_ps[b % 2], b), tiles(x, b), ALU.add))
                    dve.sem_inc(lin_free, 1)
                    dve.sem_inc(x_done, 1)


_INS = ['x', 'src', 'dst', 'edge_weight', 'L0_gnn_W', 'L0_gnn_b', 'L1_gnn_fw1', 'L1_gnn_fb1', 'L1_gnn_fw2',
        'L1_gnn_fb2', 'L1_gnn_lin1_w', 'L1_gnn_lin2_w', 'L1_gnn_lin2_b', 'L1_gnn_ln_g', 'L1_gnn_ln_b',
        'L2_gnn_gate_w', 'L2_gnn_gate_b', 'L3_gnn_W', 'L3_gnn_b']


def kernel(**inputs):
    import numpy as np
    import concourse.bacc as bacc
    from concourse.bass_utils import run_bass_kernel_spmd as run

    nc = bacc.Bacc("TRN2", target_bir_lowering=False, num_devices=1)
    arrays, args = {}, {}
    for name in _INS:
        arr = np.ascontiguousarray(inputs[name])
        arrays[f"in_{name}_dram"] = arr
        args[name] = nc.dram_tensor(f"in_{name}_dram", arr.shape, mybir.dt.from_np(arr.dtype),
                                    kind="ExternalInput").ap()
    out = nc.dram_tensor("out_0_dram", (N_NODES, D), F32, kind="ExternalOutput").ap()
    build(nc, args, out)
    r = run(nc, [arrays], core_ids=[0])
    return r.results[0]["out_0_dram"]
```
